# Optimizing a Trainium2 kernel written in Bass

```python
import numpy as np
import jax
import jax.numpy as jnp

def _softmax(x, axis=-1):
    return jax.nn.softmax(x, axis=axis)

def _gelu(x):
    return jax.nn.gelu(x, approximate=True)

def _silu(x):
    return jax.nn.silu(x)

def _sigmoid(x):
    return jax.nn.sigmoid(x)

def _layernorm(x, axis=-1, eps=1e-05):
    m = jnp.mean(x, axis=axis, keepdims=True)
    v = jnp.var(x, axis=axis, keepdims=True)
    return (x - m) / jnp.sqrt(v + eps)

def _scatter_add(tgt, idx, src, axis=0):
    return tgt.at[idx].add(src)

def _segment_sum(src, seg, n):
    return jax.ops.segment_sum(src, seg, n)
kernel_name = 'mk_decoder_preln_d1_seqx_r8_9a05ab'

def setup_inputs(seed: int=0):
    np.random.seed(seed)
    _w = jnp.asarray

    def _rec_inputs():
        import jax
        import jax.numpy as jnp
        _rk = jax.random.key(seed)
        x = 0.5 + 0.2887 * jax.random.normal(jax.random.fold_in(_rk, 1), (4, 256, 256), jnp.float32)
        _lenS = 256 - jax.random.randint(jax.random.fold_in(_rk, 7), (4,), 0, max(1, 256 // 4) + 1, jnp.int32)
        _lenS2 = 256 - jax.random.randint(jax.random.fold_in(_rk, 8), (4,), 0, max(1, 256 // 4) + 1, jnp.int32)
        _ctx_512P = jax.random.normal(jax.random.fold_in(_rk, 11), (4, 16, 64), jnp.float32)
        _ctx_512c = jax.random.dirichlet(jax.random.fold_in(_rk, 511), 0.3 * jnp.ones((16,), jnp.float32), (4, 256))
        _ctx_512t = jnp.einsum('bsk,bkd->bsd', _ctx_512c, _ctx_512P)
        _ctx_512t = _ctx_512t * jax.lax.rsqrt(jnp.mean(jnp.square(_ctx_512t)) + 1e-12) * 0.953939
        ctx_512 = -0.000392918 + 0.999932 * (_ctx_512t + 0.3 * jax.random.normal(jax.random.fold_in(_rk, 611), (4, 256, 64), jnp.float32))
        return (x, ctx_512)
    x, ctx_512 = _rec_inputs()

    def _L0_attn_setup():
        import jax, jax.numpy as jnp
        import numpy as np
        HIDDEN = 256
        HEAD_DIM = 128
        NUM_HEADS = 8
        NUM_HH = 2
        CONV = 4
        EPS = 1e-05
        KEY_DIM = NUM_HEADS * HEAD_DIM

        def _causal_conv_silu(x, w):
            y = jax.lax.conv_general_dilated(jnp.swapaxes(x, 1, 2), w, window_strides=(1,), padding=[(w.shape[-1] - 1, 0)], feature_group_count=w.shape[0], dimension_numbers=('NCH', 'OIH', 'NCH'))
            return jnp.swapaxes(jax.nn.silu(y), 1, 2)

        def _l2norm(x):
            n = jnp.sqrt(jnp.sum(x * x, axis=-1, keepdims=True))
            return x / jnp.maximum(n, 1e-12)

        def _reference_tuple_inner(x, Wq, Wk, Wv, Wb, Wa, A_log, dt_bias, conv_q_w, conv_k_w, conv_v_w, Wg, norm_w, Wo):
            B, L, _ = x.shape
            H, Dh, nh = (NUM_HEADS, HEAD_DIM, NUM_HH)
            q = _causal_conv_silu(x @ Wq, conv_q_w).reshape(B, L, H, Dh)
            k = _causal_conv_silu(x @ Wk, conv_k_w).reshape(B, L, nh, H, Dh)
            v = _causal_conv_silu(x @ Wv, conv_v_w).reshape(B, L, nh, H, Dh)
            q = _l2norm(q) / np.float32(np.sqrt(Dh))
            k = _l2norm(k)
            beta = 2.0 * jax.nn.sigmoid(x @ Wb).reshape(B, L, nh, H)
            g = -jnp.exp(A_log) * jax.nn.softplus(x @ Wa + dt_bias)

            def step(state, inp):
                q_t, k_t, v_t, b_t, g_t = inp
                state = state * jnp.exp(g_t)[..., None, None]
                for j in range(nh):
                    kj = k_t[:, j]
                    corr = jnp.einsum('bhk,bhkv->bhv', kj, state)
                    u = (v_t[:, j] - corr) * b_t[:, j][..., None]
                    state = state + jnp.einsum('bhk,bhv->bhkv', kj, u)
                o_t = jnp.einsum('bhk,bhkv->bhv', q_t, state)
                return (state, o_t)
            state0 = jnp.zeros((B, H, Dh, Dh), x.dtype)
            xs = (jnp.moveaxis(q, 1, 0), jnp.moveaxis(k, 1, 0), jnp.moveaxis(v, 1, 0), jnp.moveaxis(beta, 1, 0), jnp.moveaxis(g, 1, 0))
            state, o = jax.lax.scan(step, state0, xs)
            o = jnp.moveaxis(o, 0, 1)
            gate = (x @ Wg).reshape(B, L, H, Dh)
            o = o * jax.lax.rsqrt(jnp.mean(o * o, axis=-1, keepdims=True) + EPS)
            o = o * norm_w * jax.nn.silu(gate)
            out = o.reshape(B, L, H * Dh) @ Wo
            return (out, state)
        key = jax.random.key(seed)
        ks = jax.random.split(key, 14)
        B, L = (2, 64)
        s = 0.02
        x = jax.random.normal(ks[0], (B, L, HIDDEN), jnp.float32)
        Wq = jax.random.normal(ks[1], (HIDDEN, KEY_DIM), jnp.float32) * s
        Wk = jax.random.normal(ks[2], (HIDDEN, KEY_DIM * NUM_HH), jnp.float32) * s
        Wv = jax.random.normal(ks[3], (HIDDEN, KEY_DIM * NUM_HH), jnp.float32) * s
        Wb = jax.random.normal(ks[4], (HIDDEN, NUM_HEADS * NUM_HH), jnp.float32) * s
        Wa = jax.random.normal(ks[5], (HIDDEN, NUM_HEADS), jnp.float32) * s
        A_log = jnp.log(jax.random.uniform(ks[6], (NUM_HEADS,), jnp.float32, 0.001, 16.0))
        dt = jnp.exp(jax.random.uniform(ks[7], (NUM_HEADS,), jnp.float32) * (np.float32(np.log(0.1)) - np.float32(np.log(0.001))) + np.float32(np.log(0.001)))
        dt = jnp.maximum(dt, 0.0001)
        dt_bias = dt + jnp.log(-jnp.expm1(-dt))
        conv_q_w = jax.random.normal(ks[8], (KEY_DIM, 1, CONV), jnp.float32) * 0.1
        conv_k_w = jax.random.normal(ks[9], (KEY_DIM * NUM_HH, 1, CONV), jnp.float32) * 0.1
        conv_v_w = jax.random.normal(ks[10], (KEY_DIM * NUM_HH, 1, CONV), jnp.float32) * 0.1
        Wg = jax.random.normal(ks[11], (HIDDEN, KEY_DIM), jnp.float32) * s
        norm_w = jnp.ones((HEAD_DIM,), jnp.float32)
        Wo = jax.random.normal(ks[12], (KEY_DIM, HIDDEN), jnp.float32) * s
        return dict(x=x, Wq=Wq, Wk=Wk, Wv=Wv, Wb=Wb, Wa=Wa, A_log=A_log, dt_bias=dt_bias, conv_q_w=conv_q_w, conv_k_w=conv_k_w, conv_v_w=conv_v_w, Wg=Wg, norm_w=norm_w, Wo=Wo)
    _L0_attn_all = _L0_attn_setup()
    _L0_attn_in = {k: v for k, v in _L0_attn_all.items() if k in ('Wq', 'Wk', 'Wv', 'Wb', 'Wa', 'A_log', 'dt_bias', 'conv_q_w', 'conv_k_w', 'conv_v_w', 'Wg', 'norm_w', 'Wo')}
    del _L0_attn_all

    def _L0_xattn_setup():
        import jax, jax.numpy as jnp
        import numpy as np
        B, N, D = (16, 256, 64)
        H = 4
        TOP_K_RATIO = 0.3
        key = jax.random.key(seed)
        k1, k2, k3, k4 = jax.random.split(key, 4)
        h = jax.random.normal(k1, (B, N, D), dtype=jnp.float32)
        adj_raw = jax.random.uniform(k2, (B, N, N), dtype=jnp.float32)
        lim = 1.0 / np.sqrt(D)
        Wq = jax.random.uniform(k3, (D, D), minval=-lim, maxval=lim, dtype=jnp.float32)
        Wk = jax.random.uniform(k4, (D, D), minval=-lim, maxval=lim, dtype=jnp.float32)
        gamma_raw = jnp.float32(-0.85)
        return {'h': h, 'adj_raw': adj_raw, 'Wq': Wq, 'Wk': Wk, 'gamma_raw': gamma_raw}
    _L0_xattn_all = _L0_xattn_setup()
    _L0_xattn_in = {k: v for k, v in _L0_xattn_all.items() if k in ('Wq', 'Wk', 'gamma_raw')}
    del _L0_xattn_all

    def _L0_ffn_setup():
        import jax, jax.numpy as jnp
        import numpy as np
        H, I, E, TOP_K = (256, 704, 8, 2)

        def _silu_mul_mlp(x, w_gate_up, w_down):
            gu = x @ w_gate_up
            g, u = jnp.split(gu, 2, axis=-1)
            return jax.nn.silu(g) * u @ w_down
        key = jax.random.key(seed)
        ks = jax.random.split(key, 6)
        s = 0.02
        x = jax.random.normal(ks[0], (2, 128, H), jnp.float32)
        gate_w = jax.random.normal(ks[1], (E, H), jnp.float32) * s
        base_gate_up = jax.random.normal(ks[2], (H, 2 * I), jnp.float32) * s
        base_down = jax.random.normal(ks[3], (I, H), jnp.float32) * s
        expert_gate_up = jax.random.normal(ks[4], (E, H, 2 * I), jnp.float32) * s
        expert_down = jax.random.normal(ks[5], (E, I, H), jnp.float32) * s
        return {'x': x, 'gate_w': gate_w, 'base_gate_up': base_gate_up, 'base_down': base_down, 'expert_gate_up': expert_gate_up, 'expert_down': expert_down}
    _L0_ffn_all = _L0_ffn_setup()
    _L0_ffn_in = {k: v for k, v in _L0_ffn_all.items() if k in ('gate_w', 'base_gate_up', 'base_down', 'expert_gate_up', 'expert_down')}
    del _L0_ffn_all
    return {'x': x, 'ctx_512': ctx_512, 'L0_attn_Wq': _L0_attn_in['Wq'], 'L0_attn_Wk': _L0_attn_in['Wk'], 'L0_attn_Wv': _L0_attn_in['Wv'], 'L0_attn_Wb': _L0_attn_in['Wb'], 'L0_attn_Wa': _L0_attn_in['Wa'], 'L0_attn_A_log': _L0_attn_in['A_log'], 'L0_attn_dt_bias': _L0_attn_in['dt_bias'], 'L0_attn_conv_q_w': _L0_attn_in['conv_q_w'], 'L0_attn_conv_k_w': _L0_attn_in['conv_k_w'], 'L0_attn_conv_v_w': _L0_attn_in['conv_v_w'], 'L0_attn_Wg': _L0_attn_in['Wg'], 'L0_attn_norm_w': _L0_attn_in['norm_w'], 'L0_attn_Wo': _L0_attn_in['Wo'], 'L0_xattn_Wq': _L0_xattn_in['Wq'], 'L0_xattn_Wk': _L0_xattn_in['Wk'], 'L0_xattn_gamma_raw': _L0_xattn_in['gamma_raw'], 'L0_ffn_gate_w': _L0_ffn_in['gate_w'], 'L0_ffn_base_gate_up': _L0_ffn_in['base_gate_up'], 'L0_ffn_base_down': _L0_ffn_in['base_down'], 'L0_ffn_expert_gate_up': _L0_ffn_in['expert_gate_up'], 'L0_ffn_expert_down': _L0_ffn_in['expert_down']}

def reference(x, ctx_512, L0_attn_Wq, L0_attn_Wk, L0_attn_Wv, L0_attn_Wb, L0_attn_Wa, L0_attn_A_log, L0_attn_dt_bias, L0_attn_conv_q_w, L0_attn_conv_k_w, L0_attn_conv_v_w, L0_attn_Wg, L0_attn_norm_w, L0_attn_Wo, L0_xattn_Wq, L0_xattn_Wk, L0_xattn_gamma_raw, L0_ffn_gate_w, L0_ffn_base_gate_up, L0_ffn_base_down, L0_ffn_expert_gate_up, L0_ffn_expert_down):
    import jax
    import jax.numpy as jnp

    def _L0_attn_ref(x, Wq, Wk, Wv, Wb, Wa, A_log, dt_bias, conv_q_w, conv_k_w, conv_v_w, Wg, norm_w, Wo):
        import jax, jax.numpy as jnp
        import numpy as np
        HIDDEN = 256
        HEAD_DIM = 128
        NUM_HEADS = 8
        NUM_HH = 2
        CONV = 4
        EPS = 1e-05
        KEY_DIM = NUM_HEADS * HEAD_DIM

        def _causal_conv_silu(x, w):
            y = jax.lax.conv_general_dilated(jnp.swapaxes(x, 1, 2), w, window_strides=(1,), padding=[(w.shape[-1] - 1, 0)], feature_group_count=w.shape[0], dimension_numbers=('NCH', 'OIH', 'NCH'))
            return jnp.swapaxes(jax.nn.silu(y), 1, 2)

        def _l2norm(x):
            n = jnp.sqrt(jnp.sum(x * x, axis=-1, keepdims=True))
            return x / jnp.maximum(n, 1e-12)

        def _reference_tuple_inner(x, Wq, Wk, Wv, Wb, Wa, A_log, dt_bias, conv_q_w, conv_k_w, conv_v_w, Wg, norm_w, Wo):
            B, L, _ = x.shape
            H, Dh, nh = (NUM_HEADS, HEAD_DIM, NUM_HH)
            q = _causal_conv_silu(x @ Wq, conv_q_w).reshape(B, L, H, Dh)
            k = _causal_conv_silu(x @ Wk, conv_k_w).reshape(B, L, nh, H, Dh)
            v = _causal_conv_silu(x @ Wv, conv_v_w).reshape(B, L, nh, H, Dh)
            q = _l2norm(q) / np.float32(np.sqrt(Dh))
            k = _l2norm(k)
            beta = 2.0 * jax.nn.sigmoid(x @ Wb).reshape(B, L, nh, H)
            g = -jnp.exp(A_log) * jax.nn.softplus(x @ Wa + dt_bias)

            def step(state, inp):
                q_t, k_t, v_t, b_t, g_t = inp
                state = state * jnp.exp(g_t)[..., None, None]
                for j in range(nh):
                    kj = k_t[:, j]
                    corr = jnp.einsum('bhk,bhkv->bhv', kj, state)
                    u = (v_t[:, j] - corr) * b_t[:, j][..., None]
                    state = state + jnp.einsum('bhk,bhv->bhkv', kj, u)
                o_t = jnp.einsum('bhk,bhkv->bhv', q_t, state)
                return (state, o_t)
            state0 = jnp.zeros((B, H, Dh, Dh), x.dtype)
            xs = (jnp.moveaxis(q, 1, 0), jnp.moveaxis(k, 1, 0), jnp.moveaxis(v, 1, 0), jnp.moveaxis(beta, 1, 0), jnp.moveaxis(g, 1, 0))
            state, o = jax.lax.scan(step, state0, xs)
            o = jnp.moveaxis(o, 0, 1)
            gate = (x @ Wg).reshape(B, L, H, Dh)
            o = o * jax.lax.rsqrt(jnp.mean(o * o, axis=-1, keepdims=True) + EPS)
            o = o * norm_w * jax.nn.silu(gate)
            out = o.reshape(B, L, H * Dh) @ Wo
            return (out, state)
        return _reference_tuple_inner(x, Wq, Wk, Wv, Wb, Wa, A_log, dt_bias, conv_q_w, conv_k_w, conv_v_w, Wg, norm_w, Wo)[0]

    def _L0_xattn_ref(h, adj_raw, Wq, Wk, gamma_raw):
        import jax, jax.numpy as jnp
        import numpy as np
        B, N, D = (16, 256, 64)
        H = 4
        TOP_K_RATIO = 0.3
        b, n, dm = h.shape
        d = dm // H
        Q = (h @ Wq.T).reshape(b, n, H, d).transpose(0, 2, 1, 3)
        K = (h @ Wk.T).reshape(b, n, H, d).transpose(0, 2, 1, 3)
        sim = jnp.einsum('bhnd,bhmd->bnm', Q, K) / (jnp.sqrt(jnp.float32(d)) * H)
        k = max(1, int(n * TOP_K_RATIO))
        topk_vals = jax.lax.top_k(sim, k)[0]
        threshold = topk_vals[:, :, -1:]
        sparse_mask = (sim >= threshold).astype(sim.dtype)
        A_learned = jax.nn.sigmoid(sim) * sparse_mask
        A_learned = (A_learned + jnp.swapaxes(A_learned, -1, -2)) * 0.5
        gamma = jax.nn.sigmoid(gamma_raw)
        return (1.0 - gamma) * adj_raw + gamma * A_learned

    def _L0_ffn_ref(x, gate_w, base_gate_up, base_down, expert_gate_up, expert_down):
        import jax, jax.numpy as jnp
        import numpy as np
        H, I, E, TOP_K = (256, 704, 8, 2)

        def _silu_mul_mlp(x, w_gate_up, w_down):
            gu = x @ w_gate_up
            g, u = jnp.split(gu, 2, axis=-1)
            return jax.nn.silu(g) * u @ w_down
        B, S, Hd = x.shape
        xt = x.reshape(-1, Hd)
        base_y = _silu_mul_mlp(xt, base_gate_up, base_down)
        logits = xt @ gate_w.T
        rw = jax.nn.softmax(logits.astype(jnp.float32), axis=-1)
        top_w, top_e = jax.lax.top_k(rw, TOP_K)
        top_w = top_w / top_w.sum(axis=-1, keepdims=True)
        top_w = top_w.astype(x.dtype)
        combine = (jax.nn.one_hot(top_e, E, dtype=x.dtype) * top_w[..., None]).sum(1)
        gu = jnp.einsum('th,ehi->eti', xt, expert_gate_up)
        g, u = jnp.split(gu, 2, axis=-1)
        act = jax.nn.silu(g) * u
        out = jnp.einsum('eti,eih->eth', act, expert_down)
        moe_y = jnp.einsum('eth,te->th', out, combine)
        return (moe_y + base_y).reshape(B, S, Hd)
    x = x + _L0_attn_ref(_layernorm(x, axis=-1), L0_attn_Wq, L0_attn_Wk, L0_attn_Wv, L0_attn_Wb, L0_attn_Wa, L0_attn_A_log, L0_attn_dt_bias, L0_attn_conv_q_w, L0_attn_conv_k_w, L0_attn_conv_v_w, L0_attn_Wg, L0_attn_norm_w, L0_attn_Wo)
    x = x + _L0_xattn_ref(ctx_512, _layernorm(x, axis=-1), L0_xattn_Wq, L0_xattn_Wk, L0_xattn_gamma_raw)
    x = x + _L0_ffn_ref(_layernorm(x, axis=-1), L0_ffn_gate_w, L0_ffn_base_gate_up, L0_ffn_base_down, L0_ffn_expert_gate_up, L0_ffn_expert_down)
    return x

_drawn_inputs = setup_inputs


def setup_inputs(seed=0):
    import zlib

    import numpy as np

    out = dict(_drawn_inputs(seed))
    spreads = {'L0_attn_norm_w': (1.0, 0.6)}
    factors = {'L0_attn_Wb': 2.72,
     'L0_attn_Wa': 8.0,
     'L0_ffn_gate_w': 3.673,
     'L0_ffn_expert_gate_up': 3.194,
     'L0_ffn_expert_down': 3.202,
     'L0_ffn_base_gate_up': 2.809,
     'L0_ffn_base_down': 2.812}
    for name, (base, spread) in spreads.items():
        noise = np.random.default_rng([zlib.crc32(name.encode()), seed]).standard_normal(out[name].shape)
        drawn = base * np.exp(spread * noise) if base else spread * noise
        out[name] = jnp.asarray(drawn.astype(out[name].dtype))
    for name, factor in factors.items():
        out[name] = (out[name] * factor).astype(out[name].dtype)
    return out
```

```python
from contextlib import ExitStack

import numpy as np

import concourse.bass as bass
from concourse import mybir

F32 = mybir.dt.float32
ALU = mybir.AluOpType
ACT = mybir.ActivationFunctionType

P = 128
BATCH, SEQ, HID = 4, 256, 256
T = BATCH * SEQ
KT_H = HID // P
TT_N = T // P
HEADS, DH = 8, 128
STEPS = 64
CH = SEQ // STEPS
MU = 2 * STEPS
BC = BATCH * CH
LEVELS = 6
CONV = 4
EPS = 1e-5
CTX = 64
TOPK = int(SEQ * 0.3)
ROUNDS = -(-TOPK // 8)
LN_EXP = "natural_log_exp_and_others"
LN2 = float(np.log(2.0))
K_PROJ = 10
B_ITEMS = 20 + 12 * (LEVELS - 1) + 8


def mask_table():
    j = np.arange(P)[:, None]
    i = np.arange(P)[None, :]
    out = {"ident": (i == j), "ones": np.ones((P, P)), "strict": (i > j)}
    t = np.arange(P)[:, None]
    out["cum"] = (t <= i // 2) & (t < STEPS)
    out["rest"] = (t > i // 2) & (t < STEPS)
    out["even"] = i == 2 * t
    out["odd"] = i == 2 * t + 1
    tt = np.arange(STEPS)[None, :]
    out["upto"] = t <= tt
    out["seen"] = t // 2 <= tt
    out["neg0t"] = (i == j).astype(float) - ((j % 2 == 0) & (i == j + 1))
    for lv in range(1, LEVELS + 1):
        s = 2 ** lv
        rows, cols = j, i
        off = (rows // (2 * s) == cols // (2 * s)) & ((rows // s) % 2 == 1) & ((cols // s) % 2 == 0)
        out[f"neg{lv}"] = (i == j).astype(float) - off
    c = np.zeros((P, 16))
    c[:, 0] = 2.0 ** -60
    c[:, 1] = 15 * LN2
    c[:, 2] = 15 * LN2 - 0.5 * np.log(128.0)
    c[:, 3] = EPS
    c[:, 4] = 1.0
    c[:, 8:] = np.arange(8)
    out["scal"] = c
    return {k: v.astype(np.float32) for k, v in out.items()}


MASKS = mask_table()
MASK_AT = {}
_at = 0
for _name, _m in MASKS.items():
    MASK_AT[_name] = (_at, _m.shape[1])
    _at += _m.shape[1]
MASK_W = _at


def some(v):
    return not isinstance(v, int) or v > 0


class Head:

    def __init__(self, h, par, use):
        self.h, self.par, self.use = h, par, use


def run_heads(eng, step):
    step(Head(0, 0, 0), None, None)
    step(Head(1, 1, 0), Head(0, 0, 0), None)
    with eng.Fori(0, HEADS // 2 - 1) as m:
        step(Head(2 * m + 2, 0, m + 1), Head(2 * m + 1, 1, m), Head(2 * m, 0, m))
        step(Head(2 * m + 3, 1, m + 1), Head(2 * m + 2, 0, m + 1), Head(2 * m + 1, 1, m))
    step(None, Head(HEADS - 1, 1, HEADS // 2 - 1), Head(HEADS - 2, 0, HEADS // 2 - 1))
    step(None, None, Head(HEADS - 1, 1, HEADS // 2 - 1))


def b_items():
    out = []
    for b in range(BATCH):
        out += [("gram", b), ("qk", b), ("vtok", b)]
    out += [("x1", b) for b in range(BATCH)]
    for lv in range(1, LEVELS + 1):
        out += [("p", (lv - 1) * BATCH + b) for b in range(BATCH)]
        for b in range(BATCH):
            if lv < LEVELS:
                out.append(("x", (lv - 1) * BATCH + b))
            out.append(("xt", (lv - 1) * BATCH + b))
    out += [("kend", b) for b in range(BATCH)]
    assert len(out) == B_ITEMS
    return out


ITEMS = b_items()
QK_END = max(i for i, (kind, _) in enumerate(ITEMS) if kind == "qk") + 1
V_END = max(i for i, (kind, _) in enumerate(ITEMS) if kind == "vtok") + 1
PRE = 4 * BATCH
PER_HEAD = {k: sum(1 for kind, _ in ITEMS if kind == k) for k in ("gram", "qk", "kend", "vtok", "x1", "p", "x", "xt")}


def attention(nc, ctx, t, dram):
    sb, sem = t["sb"], t["sem"]

    masks = sb("masks", [P, MASK_W])

    def mask(name, rows=P):
        at, n = MASK_AT[name]
        return masks[0:rows, at:at + n]

    ident, ones = mask("ident"), mask("ones")
    tiny, lift_k, lift_q, eps, one = (mask("scal")[:, i:i + 1] for i in range(5))
    acc = t["acc"]
    stats = sb("stats", [P, TT_N, 6])
    mv = sb("mv", [P, TT_N, 2])
    lnv = sb("lnv", [P, TT_N])
    rstd = sb("rstd", [P, TT_N])
    xnT = sb("xnT", [P, KT_H, T])
    wab = sb("wab", [P, KT_H, 24])
    rows = sb("rows", [STEPS, 2, HEADS])
    eA = sb("eA", [STEPS, HEADS])
    g_sb = sb("g_sb", [STEPS, HEADS, BC])
    beta_sb = sb("beta_sb", [STEPS, 2, HEADS, BC])
    scal = sb("scal", [P, HEADS, 4, BC])
    cw = sb("cw", [P, HEADS, 5, CONV])
    normw = sb("normw", [P, 1])
    wbuf = [sb(f"wbuf{i}", [P, KT_H, 5, DH]) for i in range(2)]
    wo = [sb(f"wo{i}", [P, HID]) for i in range(2)]
    wg = [sb(f"wg{i}", [P, KT_H, DH]) for i in range(2)]
    cwh = [sb(f"cwh{i}", [P, 5, CONV]) for i in range(2)]
    sh = [sb(f"sh{i}", [P, 4, BC]) for i in range(2)]
    kT = [sb(f"kT{i}", [P, BATCH, CH, MU]) for i in range(2)]
    qE = [sb(f"qE{i}", [P, BATCH, CH, STEPS]) for i in range(2)]

    vtok = [sb(f"vtok{i}", [P, BATCH, CH, DH]) for i in range(2)]
    mq = [sb(f"mq{i}", [P, BATCH, CH, STEPS]) for i in range(2)]
    gate = [sb(f"gate{i}", [P, T]) for i in range(2)]
    y = [sb(f"y{i}", [P, 2, SEQ]) for i in range(2)]
    kraw = sb("kraw", [P, 2 * T])
    qraw = sb("qraw", [P, T])
    vraw = sb("vraw", [P, 2 * T])
    qT = sb("qT", [P, T])
    kend = sb("kend", [P, BATCH, CH, DH])
    osq = sb("osq", [P, T])
    sq = [osq[:, i * 512:(i + 1) * 512] for i in range(2)]
    rn = [y[i][:, :, :].rearrange("p b t -> p (b t)") for i in range(2)]
    rms = sb("rms", [P, T])
    gm = rms[0:STEPS, :].rearrange("p (n t) -> p n t", t=STEPS)
    dx = sb("dx", [P, BC, STEPS])
    ex = sb("ex", [P, BC, STEPS])
    dm = sb("dm", [P, BC, STEPS])
    aT = sb("aT", [P, BATCH, CH, MU])
    X = sb("X", [P, BATCH, CH, MU])
    XT = sb("XT", [P, BATCH, CH, MU])
    Pn = sb("Pn", [P, BATCH, CH, MU])
    TT = sb("TT", [P, BATCH, CH, MU])
    R = sb("R", [P, BATCH, DH])
    U = sb("U", [P, BATCH, DH])
    S = sb("S", [P, BATCH, DH])
    oT = sb("oT", [P, BATCH, SEQ])
    og = oT[:, :, :].rearrange("p b t -> p (b t)")

    bankA, bankB, bankC = t["banks"][0:2], t["banks"][2:6], t["banks"][6:8]

    zs = vraw[0:STEPS, 0:BC * 24].rearrange("p (n c) -> p n c", c=24)
    zt = vraw[0:STEPS, 512:512 + 768].rearrange("p (i n) -> p i n", i=3)
    flat = [w[:, :, :, :].rearrange("p b c n -> p (b c n)") for w in (X, XT, Pn)]
    hT, kcT = flat[0][0:CTX, 0:T], flat[0][0:CTX, T:2 * T]
    qcT, ctok = flat[1][0:CTX, 0:T], flat[1][:, T:T + 512]
    wqk, wqkT = flat[1][0:CTX, T + 512:T + 640], flat[1][0:CTX, T + 640:T + 768]
    simout = flat[2]
    simw = [sb(f"simw{i}", [P, SEQ]) for i in range(2)]
    m8 = sb("m8", [P, 8])
    thr = t["thr"]
    xn = kraw[:, :].rearrange("p (n d) -> p n d", n=TT_N)

    masks_in = sem("masks_in")
    x_in = sem("x_in")
    small_in = sem("small_in")
    stats_done = sem("stats_done")
    mv_done = sem("mv_done")
    lnv_done = sem("lnv_done")
    rstd_done = sem("rstd_done")
    xn_done = sem("xn_done")
    xnt_mm = sem("xnt_mm")
    xnt_done = sem("xnt_done")
    z_mm = sem("z_mm")
    z_done = sem("z_done")
    ctx_in = sem("ctx_in")
    ctx_mm = sem("ctx_mm")
    ctx_used = sem("ctx_used")
    sim_out = sem("sim_out")
    sim_in0 = sem("sim_in0")
    sim_in1 = sem("sim_in1")
    topk_step = sem("topk_step")
    sp_step = sem("sp_step")
    g_done = sem("g_done")
    beta_done = sem("beta_done")
    scal_mm = sem("scal_mm")
    scal_done = sem("scal_done")
    pre_free = sem("pre_free")
    w_in0 = sem("w_in0")
    w_in1 = sem("w_in1")
    wo_in0 = sem("wo_in0")
    wo_in1 = sem("wo_in1")
    cwh_done = sem("cwh_done")
    sh_done = sem("sh_done")
    proj_done = sem("proj_done")
    gate_mm = sem("gate_mm")
    evac_done = sem("evac_done")
    conv_step = sem("conv_step")
    silu_done = sem("silu_done")
    gate_done = sem("gate_done")
    gm_done = sem("gm_done")
    dmat_done = sem("dmat_done")
    dexp_done = sem("dexp_done")
    dm_done = sem("dm_done")
    sq_done = sem("sq_done")
    norm_mm = sem("norm_mm")
    ln_done = sem("ln_done")
    rn_done = sem("rn_done")
    kt_done = sem("kt_done")
    qe_done = sem("qe_done")
    b_mm = sem("b_mm")
    at_done = sem("at_done")
    diag_done = sem("diag_done")
    x1t_done = sem("x1t_done")
    gram_used = sem("gram_used")
    qk_used = sem("qk_used")
    kend_done = sem("kend_done")
    vtok_done = sem("vtok_done")
    x1_used = sem("x1_used")
    p_used = sem("p_used")
    x_used = sem("x_used")
    xt_used = sem("xt_used")
    ks_mm = sem("ks_mm")
    r_done = sem("r_done")
    u_mm = sem("u_mm")
    u_done = sem("u_done")
    o_mm = sem("o_mm")
    o_done = sem("o_done")
    s_mm = sem("s_mm")
    s_done = sem("s_done")
    osq_done = sem("osq_done")
    oss_mm = sem("oss_mm")
    oln_done = sem("oln_done")
    rms_done = sem("rms_done")
    og_step = sem("og_step")
    wo_mm = sem("wo_mm")
    acc_done = sem("acc_done")
    t["acc_done"] = acc_done
    sim_in = [sim_in0, sim_in1]
    w_in = [w_in0, w_in1]
    wo_in = [wo_in0, wo_in1]

    raised = {"pe": [o_mm, oss_mm, u_mm, wo_mm], "dve": [acc_done, og_step], "pool": [osq_done]}

    def raise_once(eng, who):
        for n in raised[who]:
            eng.sem_inc(n, 1)

    left = {"gram": at_done, "qk": qk_used, "kend": kend_done, "vtok": vtok_done, "x1": x1_used,
            "p": p_used, "x": x_used, "xt": xt_used}

    def a_free(pe, kind, i, h):
        if kind == "proj" and i < 2:
            if not isinstance(h, int) or h > 0:
                if some(6 * h):
                    pe.wait_ge(ln_done, 6 * h)
        elif kind == "proj":
            if some(30 * h + 3 * i - 3):
                pe.wait_ge(conv_step, 30 * h + 3 * i - 3)
        elif kind == "gate" and isinstance(h, int) and h == HEADS - 1:
            pe.wait_ge(ln_done, 6 * h + 6)
        elif kind == "gate":
            if some(30 * (h + 1) + 27 + 3 * i):
                pe.wait_ge(conv_step, 30 * (h + 1) + 27 + 3 * i)
        elif kind == "decay" and i < 2:
            pe.wait_ge(conv_step, 30 * h + 30)
            if some(2 * h):
                pe.wait_ge(gate_done, 2 * h)
        elif kind == "decay":
            if some(4 * h + i - 1):
                pe.wait_ge(dexp_done, 4 * h + i - 1)
        elif i < 2:
            pe.wait_ge(dexp_done, 4 * h + i + 3)
        else:
            if some(6 * h + i - 1):
                pe.wait_ge(ln_done, 6 * h + i - 1)

    def b_free(pe, idx, h):
        if idx >= 4:
            kind, k = ITEMS[idx - 4]
            pe.wait_ge(left[kind], PER_HEAD[kind] * h + k + 1)
        elif not isinstance(h, int) or h > 0:
            kind, k = ITEMS[idx - 4 + B_ITEMS]
            pe.wait_ge(left[kind], PER_HEAD[kind] * (h - 1) + k + 1)

    def sync_program(sp):
        sp.dma_start(ctok.rearrange("p (n d) -> p n d", d=CTX),
                     dram["ctx"].rearrange("b s d -> (b s) d").rearrange("(n p) d -> p n d", p=P)).then_inc(ctx_in, 16)
        sp.dma_start(wqk[:, 0:CTX], dram["Wcq"]).then_inc(ctx_in, 16)
        sp.dma_start(wqk[:, CTX:2 * CTX], dram["Wck"]).then_inc(ctx_in, 16)
        sp.dma_start(masks[:, :], dram["masks"]).then_inc(masks_in, 16)
        sp.dma_start(acc[:, :, :], dram["x"].rearrange("b s d -> (b s) d").rearrange("(n p) d -> p n d", p=P)).then_inc(x_in, 16)
        sp.dma_start(wab[:, :, 0:16], dram["Wb"].rearrange("(k p) n -> p k n", p=P)).then_inc(small_in, 16)
        sp.dma_start(wab[:, :, 16:24], dram["Wa"].rearrange("(k p) n -> p k n", p=P)).then_inc(small_in, 16)
        sp.dma_start(rows[:, 0, :], dram["A_log"].rearrange("(a n) -> a n", a=1).to_broadcast([STEPS, HEADS])).then_inc(small_in, 16)
        sp.dma_start(rows[:, 1, :], dram["dt_bias"].rearrange("(a n) -> a n", a=1).to_broadcast([STEPS, HEADS])).then_inc(small_in, 16)
        for i, (w, j) in enumerate((("cq", 0), ("ck", 0), ("ck", 1), ("cv", 0), ("cv", 1))):
            src = dram[w].rearrange("(j h p) a k -> j p h (a k)", p=P, h=HEADS)[j]
            sp.dma_start(cw[:, :, i, :], src).then_inc(small_in, 16)
        sp.dma_start(normw[:, :], dram["norm_w"].rearrange("(p a) -> p a", a=1)).then_inc(small_in, 16)

        for i in range(4):
            if some(8 + i):
                sp.wait_ge(ctx_used, 8 + i)
            sp.dma_start(dram["sim"][2 * i:2 * i + 2].rearrange("n p m -> p n m"),
                         simout[:, i * 512:(i + 1) * 512].rearrange("p (n m) -> p n m", n=2)).then_inc(sim_out, 16)
        sp.wait_ge(sim_out, 64)

        def step(A, B, C):
            if A:
                if not isinstance(A.h, int) or A.h >= 2:
                    if some(2 * ROUNDS * (A.h - 1)):
                        sp.wait_ge(topk_step, 2 * ROUNDS * (A.h - 1))
                sp.dma_start(simw[A.par][:, :], dram["sim"][A.h]).then_inc(sim_in[A.par], 16)
                if not isinstance(A.h, int) or A.h >= 2:
                    if some(K_PROJ * (A.h - 1)):
                        sp.wait_ge(proj_done, K_PROJ * (A.h - 1))
                for i, (w, j) in enumerate((("Wq", 0), ("Wk", 0), ("Wk", 1), ("Wv", 0), ("Wv", 1))):
                    src = dram[w].rearrange("(k p) (j h n) -> p k j h n", p=P, n=DH, h=HEADS)[:, :, j, A.h, :]
                    sp.dma_start(wbuf[A.par][:, :, i, :], src).then_inc(w_in[A.par], 16)
            if B:
                if not isinstance(B.h, int) or B.h >= 2:
                    if some(4 * (B.h - 1)):
                        sp.wait_ge(wo_mm, 4 * (B.h - 1) + 1)
                sp.dma_start(wg[B.par][:, :, :], dram["Wg"].rearrange("(k p) (h n) -> h p k n", p=P, n=DH)[B.h]).then_inc(wo_in[B.par], 16)
                sp.dma_start(wo[B.par][:, :], dram["Wo"].rearrange("(h p) n -> h p n", p=P)[B.h]).then_inc(wo_in[B.par], 16)

        run_heads(sp, step)

    PROJ = [1, 2, 0, 3, 4]

    def context_products(pe):
        mm = nc.tensor.matmul
        pe.wait_ge(ctx_in, 48)
        for i in range(11):
            bank = bankC[i % 2]
            if some(i - 1):
                pe.wait_ge(ctx_used, i - 1)
            if i < 2:
                for k in range(4):
                    last = nc.tensor.transpose(bank[0:CTX, k * P:(k + 1) * P], ctok[:, (4 * i + k) * CTX:(4 * i + k + 1) * CTX], ident)
            elif i == 2:
                for k in range(2):
                    last = nc.tensor.transpose(bank[0:CTX, k * CTX:(k + 1) * CTX], wqk[:, k * CTX:(k + 1) * CTX], ident[0:CTX, 0:CTX])
            elif i < 7:
                pe.wait_ge(ctx_used, 3)
                w, half = (i - 3) // 2, (i - 3) % 2
                last = mm(bank[0:CTX, :], wqkT[:, w * CTX:(w + 1) * CTX], hT[:, half * 512:(half + 1) * 512], start=True, stop=True)
            else:
                pe.wait_ge(ctx_used, 7)
                for k in range(2):
                    n = 2 * (i - 7) + k
                    last = mm(bank[:, k * SEQ:(k + 1) * SEQ], qcT[:, n * P:(n + 1) * P],
                              kcT[:, n // 2 * SEQ:(n // 2 + 1) * SEQ], start=True, stop=True)
            last.then_inc(ctx_mm, 1)

    def context_copies(act):
        dst = [hT[:, 0:512], hT[:, 512:T], wqkT, qcT[:, 0:512], qcT[:, 512:T], kcT[:, 0:512], kcT[:, 512:T]] \
            + [simout[:, i * 512:(i + 1) * 512] for i in range(4)]
        for i, d in enumerate(dst):
            act.wait_ge(ctx_mm, i + 1)
            rows_, cols = d.shape[0], d.shape[1]
            nc.scalar.activation(d, bankC[i % 2][0:rows_, 0:cols], ACT.Copy).then_inc(ctx_used, 1)

    def tensor_program(pe):
        mm = nc.tensor.matmul
        raise_once(pe, "pe")
        pe.wait_ge(masks_in, 16)
        context_products(pe)
        for n in range(4):
            pe.wait_ge(xn_done, 2 * n + 2)
            for k in range(4):
                tile, kt = 2 * n + k // 2, k % 2
                last = nc.tensor.transpose(bankB[n][:, k * P:(k + 1) * P], xn[:, tile, kt * P:(kt + 1) * P], ident)
            last.then_inc(xnt_mm, 1)
        pe.wait_ge(small_in, 16 * 10)
        pe.wait_ge(xnt_done, 4)
        for bc in range(BC):
            for kt in range(KT_H):
                last = mm(bankA[0][0:STEPS, bc * 24:(bc + 1) * 24], xnT[:, kt, bc * STEPS:(bc + 1) * STEPS], wab[:, kt, :],
                          start=kt == 0, stop=kt == 1)
        last.then_inc(z_mm, 1)
        pe.wait_ge(g_done, 1)
        pe.wait_ge(beta_done, 1)
        gf = g_sb[:, :, :].rearrange("p h n -> p (h n)")
        for i, m in enumerate(("cum", "rest", "ones")):
            mm(bankA[1][:, i * P:(i + 1) * P], mask(m, STEPS), gf, start=True, stop=True)
        for i, m in enumerate(("even", "odd")):
            last = mm(bankA[1][:, 3 * P:4 * P], mask(m, STEPS), beta_sb[:, i, :, :].rearrange("p h n -> p (h n)"),
                      start=i == 0, stop=i == 1)
        last.then_inc(scal_mm, 1)
        pe.wait_ge(scal_done, 4)

        def proj(A, p):
            wblk = PROJ[p // 2]
            if p == 0:
                pe.wait_ge(w_in[A.par], 5 * 16 * (A.use + 1))
            a_free(pe, "proj", p, A.h)
            for kt in range(KT_H):
                last = mm(bankA[p % 2][:, :], wbuf[A.par][:, kt, wblk, :], xnT[:, kt, (p % 2) * 512:(p % 2 + 1) * 512],
                          start=kt == 0, stop=kt == 1)
            last.then_inc(proj_done, 1)

        def gates(B):
            pe.wait_ge(wo_in[B.par], 32 * (B.use + 1))
            for i in range(2):
                a_free(pe, "gate", i, B.h)
                for kt in range(KT_H):
                    last = mm(bankA[i][:, :], wg[B.par][:, kt, :], xnT[:, kt, i * 512:(i + 1) * 512], start=kt == 0, stop=kt == 1)
                last.then_inc(gate_mm, 1)

        def decays(A):
            pe.wait_ge(gm_done, A.h + 1)
            for i in range(4):
                a_free(pe, "decay", i, A.h)
                mm(bankA[i % 2][:, :], mask("rest" if i < 2 else "ones", STEPS),
                   gm[:, (i % 2) * 8:(i % 2 + 1) * 8, :].rearrange("p n t -> p (n t)"),
                   start=True, stop=True).then_inc(dmat_done, 1)

        def norms(A):
            for i in range(6):
                pe.wait_ge(sq_done, 6 * A.h + i + 1)
                a_free(pe, "norm", i, A.h)
                mm(bankA[i % 2][:, :], ones, sq[i % 2], start=True, stop=True).then_inc(norm_mm, 1)

        def b_item(idx, B):
            kind, n = ITEMS[idx]
            b, lv = n % BATCH, n // BATCH + 1
            h, par, bank = B.h, B.par, bankB[idx % 4]
            b_free(pe, idx, h)
            if kind == "gram":
                pe.wait_ge(kt_done, 6 * h + b + 1)
            if kind == "qk" and b == 0:
                pe.wait_ge(kt_done, 6 * h + 6)
            if kind == "vtok" and b == 0:
                pe.wait_ge(silu_done, 10 * h + 10)
            if kind == "x1":
                pe.wait_ge(x1t_done, 4 * h + b + 1)
            if kind == "p":
                if lv == 1:
                    pe.wait_ge(diag_done, 8 * h + 2 * b + 2)
                    pe.wait_ge(x1_used, 4 * h + b + 1)
                else:
                    pe.wait_ge(x_used, 20 * h + (lv - 2) * BATCH + b + 1)
            if kind == "x" or (kind == "xt" and lv == LEVELS):
                pe.wait_ge(p_used, 24 * h + n + 1)
                if lv > 1:
                    if some(24 * h + n - BATCH + 1):
                        pe.wait_ge(xt_used, 24 * h + n - BATCH + 1)
            for c in range(CH):
                out = bank[:, c * P:(c + 1) * P]
                if kind == "gram":
                    last = mm(out, kT[par][:, b, c, :], kT[par][:, b, c, :], start=True, stop=True)
                elif kind == "qk":
                    at = (b * CH + c) * STEPS
                    last = mm(bank[:, c * STEPS:(c + 1) * STEPS], kT[par][:, b, c, :], qT[:, at:at + STEPS], start=True, stop=True)
                elif kind == "kend":
                    last = nc.tensor.transpose(out, kT[par][:, b, c, :], ident)
                elif kind == "vtok":
                    at = (b * CH + c) * MU
                    last = nc.tensor.transpose(out, vraw[:, at:at + MU], ident)
                elif kind == "x1":
                    last = nc.tensor.transpose(out, XT[:, b, c, :], ident)
                elif kind == "p":
                    last = mm(out, aT[:, b, c, :], X[:, b, c, :], start=True, stop=True)
                elif kind == "x":
                    last = mm(out, XT[:, b, c, :], Pn[:, b, c, :], start=True, stop=True)
                else:
                    last = mm(out, Pn[:, b, c, :], XT[:, b, c, :], start=True, stop=True)
            last.then_inc(b_mm, 1)

        def scan(C, slot):
            c, ph = slot // 3, slot % 3
            h, par = C.h, C.par
            if ph == 0 and c > 0:
                for b in range(BATCH):
                    if some(12 * h + 4 * c):
                        pe.wait_ge(s_done, 12 * h + 4 * c)
                    last = mm(bankC[0][:, b * P:(b + 1) * P], kT[par][:, b, c, :], S[:, b, :], start=True, stop=True)
                last.then_inc(ks_mm, 1)
            if ph == 1:
                if c > 0:
                    if some(4 * h + c):
                        pe.wait_ge(o_done, 4 * h + c)
                elif not isinstance(h, int) or h > 0:
                    if some(4 * h):
                        pe.wait_ge(acc_done, 4 * h + 1)
                if c == 0:
                    pe.wait_ge(xt_used, 24 * h + 24)
                for b in range(BATCH):
                    if c > 0:
                        pe.wait_ge(r_done, 12 * h + 4 * (c - 1) + b + 1)
                    last = mm(bankC[1][:, b * P:(b + 1) * P], TT[:, b, c, :], R[:, b, :] if c else vtok[par][:, b, c, :],
                              start=True, stop=True)
                last.then_inc(u_mm, 1)
            if ph == 2:
                pe.wait_ge(u_done, 4 * h + c + 1)
                if c == 0:
                    pe.wait_ge(qe_done, 2 * h + 2)
                for b in range(BATCH):
                    out = bankC[1][:, b * STEPS:(b + 1) * STEPS]
                    if c > 0:
                        mm(out, S[:, b, :], qE[par][:, b, c, :], start=True, stop=False)
                    last = mm(out, U[:, b, :], mq[par][:, b, c, :], start=c == 0, stop=True)
                last.then_inc(o_mm, 1)
                if c < CH - 1:
                    for b in range(BATCH):
                        last = mm(bankC[0][:, b * P:(b + 1) * P], kend[:, b, c, :], U[:, b, :], start=True, stop=True)
                    last.then_inc(s_mm, 1)

        def out_sums(C):
            pe.wait_ge(o_done, 4 * C.h + 4)
            pe.wait_ge(osq_done, C.h + 2)
            for i in range(2):
                mm(bankC[i][:, :], ones, osq[:, i * 512:(i + 1) * 512], start=True, stop=True).then_inc(oss_mm, 1)

        def out_proj(C):
            pe.wait_ge(og_step, 3 * C.h + 4)
            pe.wait_ge(oln_done, 2 * C.h + 2)
            for n in range(4):
                if n >= 2:
                    if some(4 * C.h + n - 1):
                        pe.wait_ge(acc_done, 4 * C.h + n)
                for k in range(2):
                    tile = 2 * n + k
                    last = mm(bankC[n % 2][:, k * HID:(k + 1) * HID], og[:, tile * P:(tile + 1) * P], wo[C.par][:, :],
                              start=True, stop=True)
                last.then_inc(wo_mm, 1)

        def step(A, B, C):
            if B:
                for idx in range(PRE):
                    b_item(idx, B)
            at = PRE
            for slot in range(12):
                if B:
                    n = 4 if slot % 2 == 0 or slot == 11 else 8
                    for idx in range(at, at + n):
                        b_item(idx, B)
                    at += n
                if C:
                    scan(C, slot)
                if A and slot < 10:
                    proj(A, slot)
                if B and slot == 10:
                    gates(B)
                if A and slot == 11:
                    decays(A)
            if C:
                out_sums(C)
            if A:
                norms(A)
            if B:
                for idx in range(at, B_ITEMS):
                    b_item(idx, B)
            if C:
                out_proj(C)

        run_heads(pe, step)

    def scalar_program(act):
        a = nc.scalar.activation
        act.wait_ge(masks_in, 16)
        context_copies(act)
        nc.scalar.preload_act_table_set(LN_EXP)
        act.wait_ge(mv_done, TT_N)
        a(lnv[:, :], mv[:, :, 1], ACT.Ln, bias=eps).then_inc(lnv_done, 1)
        act.wait_ge(lnv_done, 1)
        a(rstd[:, :], lnv[:, :], ACT.Exp, scale=-0.5).then_inc(rstd_done, 1)
        for n in range(4):
            act.wait_ge(xnt_mm, n + 1)
            a(xnT[:, :, 2 * n * P:(2 * n + 2) * P].rearrange("p k (m c) -> p m k c", m=2),
              bankB[n][:, :].rearrange("p (m k c) -> p m k c", m=2, k=2), ACT.Copy).then_inc(xnt_done, 1)
        act.wait_ge(z_mm, 1)
        act.wait_ge(small_in, 160)
        n1, n2 = BC * HEADS, BC * HEADS * 2
        a(zs[:, :, :], bankA[0][0:STEPS, 0:BC * 24].rearrange("p (n c) -> p n c", c=24), ACT.Copy).then_inc(sp_step, 1)
        act.wait_ge(sp_step, 3)
        a(zt[:, 1, 0:n1], zt[:, 1, 0:n1], ACT.Exp).then_inc(sp_step, 1)
        act.wait_ge(sp_step, 4)
        a(zt[:, 1, 0:n1], zt[:, 1, 0:n1], ACT.Ln, bias=one[0:STEPS]).then_inc(sp_step, 1)
        a(eA[:, :], rows[:, 0, :], ACT.Exp).then_inc(sp_step, 1)
        a(zt[:, 2, 0:n2].rearrange("p (n c) -> p n c", c=16), zs[:, :, 0:16], ACT.Exp, scale=-1.0).then_inc(sp_step, 1)
        act.wait_ge(scal_mm, 1)
        v = bankA[1][:, :].rearrange("p (i h n) -> p i h n", i=4, h=HEADS)
        for i, f in enumerate((ACT.Exp, ACT.Exp, ACT.Exp, ACT.Copy)):
            a(scal[:, :, i, :], v[:, i, :, :], f).then_inc(scal_done, 1)

        def evac(A, p):
            act.wait_ge(proj_done, K_PROJ * A.h + p + 1)
            if some(10 * A.h + p - 1):
                act.wait_ge(silu_done, 10 * A.h + p - 1)
            if p == 0:
                act.wait_ge(cwh_done, A.h + 1)
                if some(6 * A.h):
                    act.wait_ge(kt_done, 6 * A.h)
            cb = PROJ[p // 2]
            a(y[p % 2][:, :, :].rearrange("p b t -> p (b t)"), bankA[p % 2][:, :], ACT.Copy,
              scale=cwh[A.par][:, cb, 3:4]).then_inc(evac_done, 1)

        def silu(A, p):
            act.wait_ge(conv_step, 30 * A.h + 3 * p + 3)
            half = p % 2
            if p in (0, 4):
                if some(6 * A.h):
                    act.wait_ge(kt_done, 6 * A.h)
                if some(6 * A.h):
                    act.wait_ge(sq_done, 6 * A.h)
            if p == 6 and (not isinstance(A.h, int) or A.h > 0):
                if some(B_ITEMS * (A.h - 1) + V_END):
                    act.wait_ge(b_mm, B_ITEMS * (A.h - 1) + V_END)
            dst = {0: kraw, 1: kraw, 2: qraw, 3: vraw, 4: vraw}[p // 2]
            if p // 2 == 2:
                out = qraw[:, half * 512:(half + 1) * 512]
            else:
                out = dst[:, :].rearrange("p (t j) -> p t j", j=2)[:, half * 512:(half + 1) * 512, (0, 1, 0, 0, 1)[p // 2]]
            a(out, y[half][:, :, :].rearrange("p b t -> p (b t)"), ACT.Silu).then_inc(silu_done, 1)

        def gates(B):
            for i in range(2):
                if some(2 * B.h + 1 + i):
                    act.wait_ge(gate_mm, 2 * B.h + 1 + i)
                if not isinstance(B.h, int) or B.h >= 2:
                    if some(3 * (B.h - 1)):
                        act.wait_ge(og_step, 3 * (B.h - 1) + 1)
                a(gate[B.par][:, i * 512:(i + 1) * 512], bankA[i][:, :], ACT.Silu).then_inc(gate_done, 1)

        def decays(A):
            nc.scalar.preload_act_table_set(LN_EXP)
            for i in range(4):
                act.wait_ge(dmat_done, 4 * A.h + i + 1)
                if i == 0:
                    if some(4 * A.h):
                        act.wait_ge(at_done, 4 * A.h)
                if i == 2:
                    if some(2 * A.h):
                        act.wait_ge(qe_done, 2 * A.h)
                dst = (dx if i < 2 else ex)[:, (i % 2) * 8:(i % 2 + 1) * 8, :]
                a(dst.rearrange("p n t -> p (n t)"), bankA[i % 2][:, :], ACT.Exp).then_inc(dexp_done, 1)

        def norms(A):
            nc.scalar.preload_act_table_set(LN_EXP)
            for i in range(6):
                act.wait_ge(norm_mm, 6 * A.h + i + 1)
                if some(6 * A.h + i - 1):
                    act.wait_ge(kt_done, 6 * A.h + i - 1)
                a(rn[i % 2], bankA[i % 2][:, :], ACT.Ln, bias=tiny, scale=2.0 ** 30).then_inc(ln_done, 1)
                act.wait_ge(ln_done, 6 * A.h + i + 1)
                a(rn[i % 2], rn[i % 2], ACT.Exp, bias=lift_k if i < 4 else lift_q, scale=-0.5).then_inc(rn_done, 1)

        def copy_b(idx, B):
            kind, n = ITEMS[idx]
            b, lv = n % BATCH, n // BATCH + 1
            if kind not in ("vtok", "x1", "x", "xt"):
                return
            act.wait_ge(b_mm, B_ITEMS * B.h + idx + 1)
            if kind == "x1" and b == 0:
                act.wait_ge(sim_out, 64)
            if kind == "vtok" and b == 0 and (not isinstance(B.h, int) or B.h >= 2):
                if some(4 * (B.h - 1)):
                    act.wait_ge(u_mm, 4 * (B.h - 1) + 1)
            dst = {"vtok": vtok[B.par], "x1": X, "x": X, "xt": TT if lv == LEVELS else XT}[kind]
            a(dst[:, b, :, :].rearrange("p c n -> p (c n)"), bankB[idx % 4][:, :], ACT.Copy).then_inc(left[kind], 1)

        def scan(C, slot):
            c, ph = slot // 3, slot % 3
            if ph == 2:
                act.wait_ge(o_mm, 4 * C.h + c + 2)
                if c == 0:
                    if some(3 * C.h):
                        act.wait_ge(og_step, 3 * C.h + 1)
                    if some(C.h):
                        act.wait_ge(osq_done, C.h + 1)
                a(oT[:, :, c * STEPS:(c + 1) * STEPS], bankC[1][:, 0:BATCH * STEPS].rearrange("p (b t) -> p b t", b=BATCH),
                  ACT.Copy).then_inc(o_done, 1)

        def out_rms(C):
            nc.scalar.preload_act_table_set(LN_EXP)
            for i in range(2):
                act.wait_ge(oss_mm, 2 * C.h + i + 2)
                if some(3 * C.h):
                    act.wait_ge(og_step, 3 * C.h + 1)
                a(rms[:, i * 512:(i + 1) * 512], bankC[i][:, :], ACT.Ln, bias=eps, scale=1.0 / DH).then_inc(oln_done, 1)
            act.wait_ge(oln_done, 2 * C.h + 2)
            a(rms[:, :], rms[:, :], ACT.Exp, scale=-0.5).then_inc(rms_done, 1)

        def step(A, B, C):
            if B:
                for idx in range(PRE):
                    copy_b(idx, B)
            at = PRE
            for slot in range(12):
                if B:
                    n = 4 if slot % 2 == 0 or slot == 11 else 8
                    for idx in range(at, at + n):
                        copy_b(idx, B)
                    at += n
                if C:
                    scan(C, slot)
                if A and slot < 10:
                    evac(A, slot)
                if A and 1 <= slot <= 10:
                    silu(A, slot - 1)
                if B and slot == 10:
                    gates(B)
                if A and slot == 11:
                    decays(A)
            if C:
                out_rms(C)
            if A:
                norms(A)

        run_heads(act, step)

    def vector_program(dve):
        v = nc.vector
        raise_once(dve, "dve")
        dve.wait_ge(x_in, 16)
        for n in range(TT_N):
            v.bn_stats(stats[:, n, :], acc[:, n, :]).then_inc(stats_done, 1)
        for n in range(TT_N):
            dve.wait_ge(stats_done, n + 1)
            v.bn_aggr(mv[:, n, :], stats[:, n, :]).then_inc(mv_done, 1)
        dve.wait_ge(rstd_done, 1)
        for n in range(TT_N):
            v.tensor_scalar(xn[:, n, :], acc[:, n, :], mv[:, n, 0:1], rstd[:, n:n + 1], ALU.subtract, ALU.mult).then_inc(xn_done, 1)
        n1, n2 = BC * HEADS, BC * HEADS * 2
        dve.wait_ge(sp_step, 1)
        za = zt[:, 0, 0:n1].rearrange("p (n h) -> p n h", h=HEADS)
        v.tensor_tensor(za, zs[:, :, 16:24], rows[:, 1:2, :].to_broadcast([STEPS, BC, HEADS]), ALU.add).then_inc(sp_step, 1)
        dve.wait_ge(sp_step, 2)
        v.scalar_tensor_tensor(out=zt[:, 1, 0:n1], in0=zt[:, 0, 0:n1], scalar=-1.0, in1=zt[:, 0, 0:n1], op0=ALU.mult,
                               op1=ALU.min).then_inc(sp_step, 1)
        dve.wait_ge(sp_step, 7)
        v.scalar_tensor_tensor(out=zt[:, 0, 0:n1], in0=zt[:, 0, 0:n1], scalar=0.0, in1=zt[:, 1, 0:n1], op0=ALU.max,
                               op1=ALU.add).then_inc(sp_step, 1)
        dve.wait_ge(sp_step, 8)
        v.scalar_tensor_tensor(out=g_sb[:, :, :].rearrange("p h n -> p n h"), in0=za, scalar=-1.0,
                               in1=eA[:, :].rearrange("p (a h) -> p a h", a=1).to_broadcast([STEPS, BC, HEADS]), op0=ALU.mult,
                               op1=ALU.mult).then_inc(g_done, 1)
        v.tensor_scalar(zt[:, 2, 0:n2], zt[:, 2, 0:n2], 1.0, 0.5, ALU.add, ALU.mult).then_inc(sp_step, 1)
        dve.wait_ge(sp_step, 9)
        for j in range(2):
            v.reciprocal(beta_sb[:, j, :, :].rearrange("p h n -> p n h"),
                         zt[:, 2, 0:n2].rearrange("p (n j h) -> p n j h", j=2, h=HEADS)[:, :, j, :]).then_inc(
                sp_step if j == 0 else beta_done, 1)
        dve.wait_ge(sp_step, 10)

        def conv(A, p):
            dve.wait_ge(evac_done, 10 * A.h + p + 1)
            cb = PROJ[p // 2]
            src = bankA[p % 2][:, :].rearrange("p (b t) -> p b t", b=2)
            for k in range(1, CONV):
                if k > 1:
                    topk(A, 2 * p + k - 2)
                    if some(30 * A.h + 3 * p + k - 1):
                        dve.wait_ge(conv_step, 30 * A.h + 3 * p + k - 1)
                if k < 3:
                    if some(2 * ROUNDS * A.h + 2 * p + k - 1):
                        dve.wait_ge(topk_step, 2 * ROUNDS * A.h + 2 * p + k - 1)
                if k == 1 and p == 0:
                    dve.wait_ge(sim_in[A.par], 16 * (A.use + 1))
                v.scalar_tensor_tensor(out=y[p % 2][:, :, k:], in0=src[:, :, 0:SEQ - k], scalar=cwh[A.par][:, cb, 3 - k:4 - k],
                                       in1=y[p % 2][:, :, k:], op0=ALU.mult, op1=ALU.add).then_inc(conv_step, 1)

        def topk(A, k):
            w = simw[A.par][:, :]
            if k == 2 * ROUNDS - 1:
                at = (TOPK - 1) % 8
                ins = v.tensor_copy(thr[:, A.h:A.h + 1] if isinstance(A.h, int) else thr[:, bass.ds(A.h, 1)], m8[:, at:at + 1])
            elif k % 2 == 0:
                ins = v.max(out=m8[:, :], in_=w)
            else:
                ins = v.match_replace(out=w, in_to_replace=m8[:, :], in_values=w, imm_value=-3.0e38)
            ins.then_inc(topk_step, 1)

        def norms(A):
            for i in range(6):
                dve.wait_ge(rn_done, 6 * A.h + i + 1)
                if i < 4:
                    if i == 0 and (not isinstance(A.h, int) or A.h >= 2):
                        if some(3 * (A.h - 1)):
                            dve.wait_ge(ks_mm, 3 * (A.h - 1))
                    src, dst = kraw[:, i * 512:(i + 1) * 512], kT[A.par][:, i, :, :].rearrange("p c n -> p (c n)")
                else:
                    if i == 4 and (not isinstance(A.h, int) or A.h >= 1):
                        if some(B_ITEMS * (A.h - 1) + QK_END):
                            dve.wait_ge(b_mm, B_ITEMS * (A.h - 1) + QK_END)
                        if some(2 * A.h):
                            dve.wait_ge(qe_done, 2 * A.h)
                    src, dst = qraw[:, (i - 4) * 512:(i - 3) * 512], qT[:, (i - 4) * 512:(i - 3) * 512]
                top = 1e12 if i < 4 else 1e12 / float(np.sqrt(DH))
                v.scalar_tensor_tensor(out=dst, in0=rn[i % 2], scalar=top, in1=src, op0=ALU.min, op1=ALU.mult).then_inc(kt_done, 1)

        def evac_b(idx, B):
            kind, n = ITEMS[idx]
            b, lv = n % BATCH, n // BATCH + 1
            if kind not in ("gram", "qk", "kend", "p"):
                return
            dve.wait_ge(b_mm, B_ITEMS * B.h + idx + 1)
            bank = bankB[idx % 4][:, :]
            if kind == "gram":
                if b == 0:
                    dve.wait_ge(dm_done, 2 * B.h + 2)
                v.tensor_tensor(aT[:, b, :, :].rearrange("p c (t j) -> p (c t) j", j=2), bank.rearrange("p (t j) -> p t j", j=2),
                                dx[:, b * CH:(b + 1) * CH, :].rearrange("p c (n a) -> p (c n) a", a=1).to_broadcast([P, CH * STEPS, 2]),
                                ALU.mult).then_inc(at_done, 1)
            elif kind == "qk":
                if b == 0 and (not isinstance(B.h, int) or B.h >= 2):
                    if some(4 * (B.h - 1)):
                        dve.wait_ge(o_mm, 4 * (B.h - 1) + 1)
                v.tensor_tensor(mq[B.par][:, b, :, :].rearrange("p c n -> p (c n)"), bank[:, 0:CH * STEPS],
                                dm[:, b * CH:(b + 1) * CH, :].rearrange("p c n -> p (c n)"), ALU.mult).then_inc(qk_used, 1)
            elif kind == "kend":
                if b == 0:
                    dve.wait_ge(sh_done, B.h + 1)
                v.tensor_tensor(kend[:, b, :, :], bank.rearrange("p (c n) -> p c n", c=CH),
                                sh[B.par][:, 1, b * CH:(b + 1) * CH].rearrange("p (c a) -> p c a", a=1).to_broadcast([P, CH, DH]),
                                ALU.mult).then_inc(kend_done, 1)
            else:
                v.tensor_tensor(Pn[:, b, :, :], bank.rearrange("p (c n) -> p c n", c=CH),
                                mask(f"neg{lv}").rearrange("p (a n) -> p a n", a=1).to_broadcast([P, CH, MU]),
                                ALU.mult).then_inc(p_used, 1)

        def scan(C, slot):
            c, ph = slot // 3, slot % 3
            h, par = C.h, C.par
            if ph == 0 and c > 0:
                if some(3 * h + c):
                    dve.wait_ge(ks_mm, 3 * h + c)
                for b in range(BATCH):
                    v.scalar_tensor_tensor(out=R[:, b, :], in0=bankC[0][:, b * P:(b + 1) * P],
                                           scalar=sh[par][:, 0, b * CH + c:b * CH + c + 1], in1=vtok[par][:, b, c, :],
                                           op0=ALU.mult, op1=ALU.add).then_inc(r_done, 1)
            if ph == 1:
                dve.wait_ge(u_mm, 4 * h + c + 2)
                if c == 0:
                    if some(4 * h):
                        dve.wait_ge(o_mm, 4 * h + 1)
                v.tensor_tensor(U[:, :, :], bankC[1][:, :].rearrange("p (b n) -> p b n", b=BATCH),
                                sh[par][:, 3, :].rearrange("p (b c a) -> p b c a", b=BATCH, a=1)[:, :, c, :].to_broadcast([P, BATCH, DH]),
                                ALU.mult).then_inc(u_done, 1)
            if ph == 2 and c < CH - 1:
                dve.wait_ge(s_mm, 3 * h + c + 1)
                for b in range(BATCH):
                    if c == 0:
                        v.tensor_copy(S[:, b, :], bankC[0][:, b * P:(b + 1) * P]).then_inc(s_done, 1)
                    else:
                        v.scalar_tensor_tensor(out=S[:, b, :], in0=S[:, b, :], scalar=sh[par][:, 2, b * CH + c:b * CH + c + 1],
                                               in1=bankC[0][:, b * P:(b + 1) * P], op0=ALU.mult, op1=ALU.add).then_inc(s_done, 1)

        def out_gate(C):
            h = C.h
            dve.wait_ge(osq_done, h + 2)
            v.scalar_tensor_tensor(out=og[:, :], in0=oT[:, :, :].rearrange("p b t -> p (b t)"), scalar=normw[:, 0:1],
                                   in1=gate[C.par][:, :], op0=ALU.mult, op1=ALU.mult).then_inc(og_step, 1)
            dve.wait_ge(rms_done, h + 1)
            dve.wait_ge(og_step, 3 * h + 2)
            for i in range(2):
                v.tensor_tensor(og[:, i * 512:(i + 1) * 512], og[:, i * 512:(i + 1) * 512], rms[:, i * 512:(i + 1) * 512],
                                ALU.mult).then_inc(og_step, 1)

        def out_add(C):
            for n in range(4):
                dve.wait_ge(wo_mm, 4 * C.h + n + 2)
                v.tensor_tensor(acc[:, 2 * n:2 * n + 2, :].rearrange("p k d -> p (k d)"), acc[:, 2 * n:2 * n + 2, :].rearrange("p k d -> p (k d)"),
                                bankC[n % 2][:, :], ALU.add).then_inc(acc_done, 1)

        def step(A, B, C):
            if B:
                for idx in range(PRE):
                    evac_b(idx, B)
            at = PRE
            for slot in range(12):
                if B:
                    n = 4 if slot % 2 == 0 or slot == 11 else 8
                    for idx in range(at, at + n):
                        evac_b(idx, B)
                    at += n
                if C:
                    scan(C, slot)
                if A and slot < 10:
                    conv(A, slot)
            if C:
                dve.wait_ge(o_done, 4 * C.h + 4)
                out_gate(C)
            if A:
                norms(A)
            if B:
                for idx in range(at, B_ITEMS):
                    evac_b(idx, B)
            if C:
                out_add(C)

        run_heads(dve, step)

    def gpsimd_program(pool):
        g = nc.gpsimd
        raise_once(pool, "pool")
        pool.wait_ge(masks_in, 16)
        pool.wait_ge(small_in, 160)
        pool.wait_ge(scal_done, 4)
        g.tensor_scalar(scal[:, :, 0, :], scal[:, :, 0, :], -1.0, None, ALU.mult).then_inc(scal_done, 1)
        pool.wait_ge(scal_done, 5)

        def start(A):
            h = A.h
            if not isinstance(h, int) or h >= 2:
                if some(30 * (h - 1)):
                    pool.wait_ge(conv_step, 30 * (h - 1))
            g.tensor_copy(cwh[A.par][:, :, :].rearrange("p a k -> p (a k)"),
                          cw[:, :, :, :].rearrange("p h a k -> p h (a k)")[:, h, :]).then_inc(cwh_done, 1)
            if some(4 * h):
                pool.wait_ge(dmat_done, 4 * h)
            if not isinstance(h, int) or h > 2:
                if some(3 * (h - 2)):
                    pool.wait_ge(og_step, 3 * (h - 2) + 1)
            g.tensor_tensor(gm[:, :, :], g_sb[:, h, :].rearrange("p (n a) -> p n a", a=1).to_broadcast([STEPS, BC, STEPS]),
                            mask("upto", STEPS).rearrange("p (a n) -> p a n", a=1).to_broadcast([STEPS, BC, STEPS]),
                            ALU.mult).then_inc(gm_done, 1)

        def squares(A, i):
            if some(10 * A.h + (4 if i < 4 else 6)):
                pool.wait_ge(silu_done, 10 * A.h + (4 if i < 4 else 6))
            if some(6 * A.h + i - 1):
                pool.wait_ge(norm_mm, 6 * A.h + i - 1)
            if i == 0 and (not isinstance(A.h, int) or A.h >= 2):
                if some(2 * (A.h - 1)):
                    pool.wait_ge(oss_mm, 2 * (A.h - 1) + 1)
            src = kraw[:, i * 512:(i + 1) * 512] if i < 4 else qraw[:, (i - 4) * 512:(i - 3) * 512]
            g.tensor_tensor(sq[i % 2], src, src, ALU.mult).then_inc(sq_done, 1)

        def decays(A):
            h = A.h
            if not isinstance(h, int) or h >= 2:
                if some(12 * (h - 1)):
                    pool.wait_ge(r_done, 12 * (h - 1))
                if some(4 * (h - 1)):
                    pool.wait_ge(u_done, 4 * (h - 1))
                if some(12 * (h - 1)):
                    pool.wait_ge(s_done, 12 * (h - 1))
            g.tensor_copy(sh[A.par][:, :, :].rearrange("p a k -> p (a k)"),
                          scal[:, :, :, :].rearrange("p h a k -> p h (a k)")[:, h, :]).then_inc(sh_done, 1)
            pool.wait_ge(dexp_done, 4 * h + 2)
            if some(4 * h):
                pool.wait_ge(qk_used, 4 * h)
            pool.wait_ge(sh_done, h + 1)
            g.tensor_tensor(dm[:, :, :], dx[:, :, :], mask("seen").rearrange("p (a n) -> p a n", a=1).to_broadcast([P, BC, STEPS]),
                            ALU.mult).then_inc(dm_done, 1)
            pool.wait_ge(dm_done, 2 * h + 1)
            g.tensor_tensor(dx[:, :, :], dx[:, :, :], sh[A.par][:, 3, :].rearrange("p (n a) -> p n a", a=1).to_broadcast([P, BC, STEPS]),
                            ALU.mult).then_inc(dm_done, 1)

        def q_decay(A):
            for i in range(2):
                if some(6 * A.h + 5 + i):
                    pool.wait_ge(kt_done, 6 * A.h + 5 + i)
                if i == 0:
                    pool.wait_ge(dexp_done, 4 * A.h + 4)
                    if not isinstance(A.h, int) or A.h >= 2:
                        if some(4 * (A.h - 1)):
                            pool.wait_ge(o_mm, 4 * (A.h - 1) + 1)
                g.tensor_tensor(qE[A.par][:, 2 * i:2 * i + 2, :, :].rearrange("p b c t -> p (b c t)"), qT[:, i * 512:(i + 1) * 512],
                                ex[:, i * 8:(i + 1) * 8, :].rearrange("p n t -> p (n t)"), ALU.mult).then_inc(qe_done, 1)

        def diag(B, b):
            pool.wait_ge(at_done, 4 * B.h + b + 1)
            g.tensor_tensor(aT[:, b, :, :], aT[:, b, :, :], mask("strict").rearrange("p (a n) -> p a n", a=1).to_broadcast([P, CH, MU]),
                            ALU.mult).then_inc(diag_done, 1)
            pool.wait_ge(diag_done, 8 * B.h + 2 * b + 1)
            g.tensor_tensor(aT[:, b, :, :], aT[:, b, :, :], ident.rearrange("p (a n) -> p a n", a=1).to_broadcast([P, CH, MU]),
                            ALU.add).then_inc(diag_done, 1)
            pool.wait_ge(diag_done, 8 * B.h + 2 * b + 2)
            if not isinstance(B.h, int) or B.h > 0:
                if some(B_ITEMS * B.h):
                    pool.wait_ge(b_mm, B_ITEMS * B.h)
            else:
                pool.wait_ge(sim_out, 64)
            g.tensor_tensor(XT[:, b, :, :], aT[:, b, :, :], mask("neg0t").rearrange("p (a n) -> p a n", a=1).to_broadcast([P, CH, MU]),
                            ALU.mult).then_inc(x1t_done, 1)

        def step(A, B, C):
            if B:
                for b in range(BATCH):
                    diag(B, b)
            if A:
                start(A)
            if A:
                decays(A)
            if C:
                pool.wait_ge(o_done, 4 * C.h + 4)
                if some(2 * C.h):
                    pool.wait_ge(oss_mm, 2 * C.h + 1)
                g.tensor_tensor(osq[:, :], oT[:, :, :].rearrange("p b t -> p (b t)"), oT[:, :, :].rearrange("p b t -> p (b t)"),
                                ALU.mult).then_inc(osq_done, 1)
            if A:
                for i in range(6):
                    squares(A, i)
                q_decay(A)

        run_heads(pool, step)

    return {"sync": sync_program, "pe": tensor_program, "act": scalar_program, "dve": vector_program, "pool": gpsimd_program}


FF, EXPERTS = 704, 8
FFH = FF // 2
FT = -(-FF // P)
FT_ROWS = [min(P, FF - k * P) for k in range(FT)]
WAYS = EXPERTS + 1


def feed_forward(nc, t, dram):
    sb, sem, acc, thr = t["sb"], t["sem"], t["acc"], t["thr"]
    gu = t["banks"][0:4]
    tr = t["banks"][4:6]
    dn = t["banks"][6:8]

    masks = sb("f_masks", [P, MASK_W])
    at, _ = MASK_AT["ident"]
    ident = masks[:, at:at + P]
    at, _ = MASK_AT["scal"]
    eps = masks[:, at + 3:at + 4]
    iota = masks[:, at + 8:at + 16]
    stats = sb("f_stats", [P, TT_N, 6])
    mv = sb("f_mv", [P, 2, TT_N, 2])
    lnv = sb("f_lnv", [P, TT_N])
    rstd = sb("f_rstd", [P, 2, TT_N])
    gam = sb("f_gam", [P, 4])
    small = sb("f_small", [P, 4, TT_N])
    gwT = sb("f_gwT", [P, KT_H, EXPERTS])
    gw = sb("f_gw", [EXPERTS, HID])
    lg = sb("f_lg", [P, TT_N, EXPERTS])
    top = sb("f_top", [P, TT_N, 8])
    idx = sb("f_idx", [P, TT_N, 8], mybir.dt.uint32)
    idxf = sb("f_idxf", [P, TT_N, 8])
    hot = sb("f_hot", [P, 2, TT_N, EXPERTS])
    comb = sb("f_comb", [P, TT_N, WAYS])
    x2T = sb("f_x2T", [P, KT_H, T])
    sg = sb("f_sg", [P, 2, FFH])
    av = sb("f_act", [P, 2, FF])
    aT = sb("f_actT", [P, 2, FT, P])
    wgu = sb("f_wgu", [P, WAYS, KT_H, 2 * FF])
    wdn = sb("f_wdn", [P, WAYS, FT, HID])
    last_w = wgu[:, WAYS - 1, :, :].rearrange("p k n -> p (k n)")
    prev_w = wgu[:, WAYS - 2, :, :].rearrange("p k n -> p (k n)")
    third_w = wgu[:, WAYS - 3, :, :].rearrange("p k n -> p (k n)")
    simb = last_w[:, 0:2048].rearrange("p (n m) -> p n m", n=TT_N)
    am = prev_w[:, 0:2048].rearrange("p (n m) -> p n m", n=TT_N)
    xn2 = third_w[:, 0:2048].rearrange("p (n m) -> p n m", n=TT_N)

    f_in = sem("f_in")
    f_sim_in = sem("f_sim_in")
    f_gw_in = sem("f_gw_in")
    f_sig = sem("f_sig")
    f_gam = sem("f_gam")
    f_am = sem("f_am")
    f_tr_mm = sem("f_tr_mm")
    f_ls = sem("f_ls")
    f_mv = sem("f_mv")
    f_rstd = sem("f_rstd")
    f_x2 = sem("f_x2")
    f_ln2 = sem("f_ln2")
    f_xn2 = sem("f_xn2")
    f_x2t_mm = sem("f_x2t_mm")
    f_x2t = sem("f_x2t")
    f_gwt_mm = sem("f_gwt_mm")
    f_gwt = sem("f_gwt")
    f_lg_mm = sem("f_lg_mm")
    f_route = sem("f_route")
    f_exp = sem("f_exp")
    f_comb = sem("f_comb")
    f_w_landed = sem("f_w_landed")
    f_gu_mm = sem("f_gu_mm")
    f_silu = sem("f_silu")
    f_act = sem("f_act")
    f_at_mm = sem("f_at_mm")
    f_at = sem("f_at")
    f_dn_mm = sem("f_dn_mm")
    f_add = sem("f_add")
    f_out = sem("f_out")
    w_dma = [sem(f"f_w{i}") for i in range(WAYS)]

    def free(eng):
        eng.wait_ge(t["acc_done"], 4 * HEADS + 1)

    def sync_program(sp):
        free(sp)
        sp.dma_start(masks[:, :], dram["masks"]).then_inc(f_in, 16)
        sp.dma_start(gam[:, 0:1], dram["gamma"].rearrange("(a n) -> a n", a=1).to_broadcast([P, 1])).then_inc(f_in, 16)
        sp.dma_start(simb, dram["sim"].rearrange("n p m -> p n m")).then_inc(f_sim_in, 16)
        sp.dma_start(gw[:, :], dram["gate_w"]).then_inc(f_gw_in, 16)
        for e in range(WAYS):
            if e == WAYS - 3:
                sp.wait_ge(f_x2t, 8)
            if e == WAYS - 2:
                sp.wait_ge(f_x2, 2 * TT_N)
            g = dram["base_gu"] if e == 0 else dram["exp_gu"][e - 1]
            d = dram["base_dn"] if e == 0 else dram["exp_dn"][e - 1]
            sp.dma_start(wgu[:, e, :, :], g.rearrange("(k p) n -> p k n", p=P)).then_inc(w_dma[e], 16)
            full = FT - 1
            sp.dma_start(wdn[:, e, 0:full, :], d[0:full * P].rearrange("(k p) n -> p k n", p=P)).then_inc(w_dma[e], 16)
            sp.dma_start(wdn[0:FT_ROWS[-1], e, full, :], d[full * P:FF]).then_inc(w_dma[e], 16)
            if e >= 1:
                sp.wait_ge(w_dma[e - 1], 48)
                sp.sem_inc(f_w_landed, 1)
        sp.wait_ge(w_dma[WAYS - 1], 48)
        sp.sem_inc(f_w_landed, 1)
        for n in range(TT_N):
            sp.wait_ge(f_add, (WAYS - 1) * TT_N + n + 1)
            sp.dma_start(dram["out"].rearrange("b s d -> (b s) d")[n * P:(n + 1) * P], acc[:, n, :]).then_inc(f_out, 16)
        sp.wait_ge(f_out, 16 * TT_N)

    def tensor_program(pe):
        mm = nc.tensor.matmul
        free(pe)
        pe.wait_ge(f_in, 32)
        for n in range(TT_N):
            pe.wait_ge(f_am, 2 * (n // 2) + 2)
            if n >= 2:
                if some(n - 1):
                    pe.wait_ge(f_ls, n - 1)
            for k in range(2):
                src = am[:, n // 2 * 2 + k, (n % 2) * P:(n % 2 + 1) * P]
                last = nc.tensor.transpose(tr[n % 2][:, k * P:(k + 1) * P], src, ident)
            last.then_inc(f_tr_mm, 1)
        pe.wait_ge(f_gw_in, 16)
        for k in range(KT_H):
            last = nc.tensor.transpose(dn[0][:, k * EXPERTS:(k + 1) * EXPERTS], gw[:, k * P:(k + 1) * P], ident[0:EXPERTS, 0:EXPERTS])
        last.then_inc(f_gwt_mm, 1)
        for n in range(TT_N):
            pe.wait_ge(f_xn2, n + 1)
            if n < 2:
                if some(TT_N - 1 + n):
                    pe.wait_ge(f_ls, TT_N - 1 + n)
            else:
                if some(n - 1):
                    pe.wait_ge(f_x2t, n - 1)
            for k in range(KT_H):
                last = nc.tensor.transpose(tr[n % 2][:, k * P:(k + 1) * P], xn2[:, n, k * P:(k + 1) * P], ident)
            last.then_inc(f_x2t_mm, 1)
        pe.wait_ge(f_gwt, 1)
        pe.wait_ge(f_x2t, TT_N)
        for n in range(TT_N):
            for k in range(KT_H):
                last = mm(dn[1][:, n * EXPERTS:(n + 1) * EXPERTS], x2T[:, k, n * P:(n + 1) * P], gwT[:, k, :], start=k == 0, stop=k == 1)
        last.then_inc(f_lg_mm, 1)

        def gate_up(e, n):
            job = e * TT_N + n
            if n == 0:
                pe.wait_ge(f_w_landed, e + 1)
            for c in range(4):
                at = (c % 2) * FF + (c // 2) * FFH
                if isinstance(e, int) and e == 0 and n == 0:
                    pass
                else:
                    if some(2 * job - 1 + c // 2):
                        pe.wait_ge(f_act, 2 * job - 1 + c // 2)
                for k in range(KT_H):
                    last = mm(gu[c][:, 0:FFH], x2T[:, k, n * P:(n + 1) * P], wgu[:, e, k, at:at + FFH], start=k == 0, stop=k == 1)
                last.then_inc(f_gu_mm, 1)

        def down(e, n):
            job = e * TT_N + n
            pe.wait_ge(f_act, 2 * job + 2)
            for half in range(2):
                if isinstance(e, int) and job == 0:
                    pass
                else:
                    if some(2 * job - 1 + half):
                        pe.wait_ge(f_at, 2 * job - 1 + half)
                for k in range(3 * half, 3 * half + 3):
                    rows = FT_ROWS[k]
                    last = nc.tensor.transpose(tr[half][0:rows, (k % 3) * P:(k % 3 + 1) * P], av[:, n % 2, k * P:k * P + rows], ident)
                last.then_inc(f_at_mm, 1)
            if isinstance(e, int) and job == 0:
                pe.wait_ge(f_gwt, 1)
            elif isinstance(e, int) and job == 1:
                pe.wait_ge(f_route, 1)
            else:
                if some(job - 1):
                    pe.wait_ge(f_add, job - 1)
            pe.wait_ge(f_at, 2 * job + 2)
            for k in range(FT):
                rows = FT_ROWS[k]
                last = mm(dn[n % 2][:, 0:HID], aT[0:rows, n % 2, k, :], wdn[0:rows, e, k, :], start=k == 0, stop=k == FT - 1)
            last.then_inc(f_dn_mm, 1)

        def one_set(e):
            for n in range(TT_N):
                if n < TT_N - 1:
                    gate_up(e, n + 1)
                elif not isinstance(e, int) or e < WAYS - 1:
                    gate_up(e + 1, 0)
                down(e, n)

        gate_up(0, 0)
        one_set(0)
        with pe.Fori(1, WAYS - 1) as e:
            one_set(e)
        one_set(WAYS - 1)

    def scalar_program(act):
        a = nc.scalar.activation
        free(act)
        act.wait_ge(f_in, 32)
        act.wait_ge(f_sim_in, 16)
        a(am, simb, ACT.Sigmoid, scale=1.0 / 16).then_inc(f_sig, 1)
        a(gam[:, 1:2], gam[:, 0:1], ACT.Sigmoid).then_inc(f_gam, 1)
        nc.scalar.preload_act_table_set(LN_EXP)

        def inv_std(i):
            if some(TT_N * (i + 1)):
                act.wait_ge(f_mv, TT_N * (i + 1))
            a(lnv[:, :], mv[:, i, :, 1], ACT.Ln, bias=eps).then_inc(f_rstd, 1)
            act.wait_ge(f_rstd, 2 * i + 1)
            a(rstd[:, i, :], lnv[:, :], ACT.Exp, scale=-0.5).then_inc(f_rstd, 1)

        inv_std(0)
        act.wait_ge(f_gwt_mm, 1)
        a(gwT[:, :, :].rearrange("p k n -> p (k n)"), dn[0][:, 0:KT_H * EXPERTS], ACT.Copy).then_inc(f_gwt, 1)
        inv_std(1)
        for n in range(TT_N):
            act.wait_ge(f_x2t_mm, n + 1)
            a(x2T[:, :, n * P:(n + 1) * P], tr[n % 2][:, 0:HID].rearrange("p (k c) -> p k c", k=KT_H), ACT.Copy).then_inc(f_x2t, 1)
        act.wait_ge(f_route, 2)
        a(small[:, 1, :], small[:, 0, :], ACT.Exp).then_inc(f_exp, 1)

        def silu(e, n):
            for half in range(2):
                act.wait_ge(f_gu_mm, 4 * (e * TT_N + n) + 2 * half + 1)
                if isinstance(e, int) and e * TT_N + n == 0:
                    pass
                else:
                    if some(2 * (e * TT_N + n) - 1 + half):
                        act.wait_ge(f_act, 2 * (e * TT_N + n) - 1 + half)
                a(sg[:, half, :], gu[2 * half][:, 0:FFH], ACT.Silu).then_inc(f_silu, 1)

        def copy_t(e, n):
            for half in range(2):
                act.wait_ge(f_at_mm, 2 * (e * TT_N + n) + half + 1)
                if half == 0:
                    if not isinstance(e, int) or e * TT_N + n >= 2:
                        if some(e * TT_N + n - 1):
                            act.wait_ge(f_dn_mm, e * TT_N + n - 1)
                    a(aT[:, n % 2, 0:3, :].rearrange("p k c -> p (k c)"), tr[0][:, 0:3 * P], ACT.Copy).then_inc(f_at, 1)
                else:
                    a(aT[:, n % 2, 3:5, :].rearrange("p k c -> p (k c)"), tr[1][:, 0:2 * P], ACT.Copy)
                    a(aT[0:FT_ROWS[-1], n % 2, 5, :], tr[1][0:FT_ROWS[-1], 2 * P:3 * P], ACT.Copy).then_inc(f_at, 1)

        def one_set(e):
            for n in range(TT_N):
                if n < TT_N - 1:
                    silu(e, n + 1)
                elif not isinstance(e, int) or e < WAYS - 1:
                    silu(e + 1, 0)
                copy_t(e, n)

        silu(0, 0)
        one_set(0)
        with act.Fori(1, WAYS - 1) as e:
            one_set(e)
        one_set(WAYS - 1)

    def vector_program(dve):
        v = nc.vector
        free(dve)
        chain = sem("f_chain")
        count = [0]

        def link(ins):
            count[0] += 1
            ins.then_inc(chain, 1)
            dve.wait_ge(chain, count[0])

        def moments(i, n):
            link(v.bn_stats(stats[:, n, :], acc[:, n, :]))
            v.bn_aggr(mv[:, i, n, :], stats[:, n, :]).then_inc(f_mv, 1)

        for n in range(TT_N):
            moments(0, n)
        dve.wait_ge(f_gam, 1)
        link(v.tensor_scalar(gam[:, 2:3], gam[:, 1:2], 0.5, None, ALU.mult))
        link(v.tensor_scalar(gam[:, 3:4], gam[:, 1:2], -1.0, 1.0, ALU.mult, ALU.add))
        dve.wait_ge(f_sig, 1)
        for n in range(TT_N):
            v.scalar_tensor_tensor(out=am[:, n, :], in0=simb[:, n, :], scalar=thr[:, n:n + 1], in1=am[:, n, :], op0=ALU.is_ge,
                                   op1=ALU.mult).then_inc(f_am, 1)
        dve.wait_ge(f_am, TT_N)
        for n in range(TT_N):
            dve.wait_ge(f_tr_mm, n + 1)
            v.tensor_tensor(simb[:, n, :], am[:, n, :], tr[n % 2][:, 0:SEQ], ALU.add).then_inc(f_ls, 1)
        dve.wait_ge(f_ls, TT_N)
        dve.wait_ge(f_rstd, 2)
        link(v.tensor_scalar(small[:, 0, :], rstd[:, 0, :], gam[:, 3:4], None, ALU.mult))
        link(v.tensor_tensor(small[:, 2, :], small[:, 0, :], mv[:, 0, :, 0], ALU.mult))
        for n in range(TT_N):
            link(v.tensor_scalar(xn2[:, n, :], acc[:, n, :], mv[:, 0, n, 0:1], small[:, 0, n:n + 1], ALU.subtract, ALU.mult))
            link(v.scalar_tensor_tensor(out=xn2[:, n, :], in0=simb[:, n, :], scalar=gam[:, 2:3], in1=xn2[:, n, :], op0=ALU.mult, op1=ALU.add))
            v.tensor_tensor(acc[:, n, :], acc[:, n, :], xn2[:, n, :], ALU.add).then_inc(f_x2, 2)
            dve.wait_ge(f_x2, 2 * n + 2)
            moments(1, n)
        dve.wait_ge(f_mv, 2 * TT_N)
        dve.wait_ge(f_rstd, 4)
        for n in range(TT_N):
            v.tensor_scalar(xn2[:, n, :], acc[:, n, :], mv[:, 1, n, 0:1], rstd[:, 1, n:n + 1], ALU.subtract, ALU.mult).then_inc(f_xn2, 1)
        dve.wait_ge(f_lg_mm, 1)
        v.tensor_copy(lg[:, :, :].rearrange("p n e -> p (n e)"), dn[1][:, 0:TT_N * EXPERTS]).then_inc(f_route, 1)
        dve.wait_ge(f_route, 1)
        for n in range(TT_N):
            last = v.max(out=top[:, n, :], in_=lg[:, n, :])
        link(last)
        v.tensor_tensor(small[:, 0, :], top[:, :, 1], top[:, :, 0], ALU.subtract).then_inc(f_route, 1)
        for n in range(TT_N):
            last = v.max_index(out=idx[:, n, :], in_max=top[:, n, :], in_values=lg[:, n, :])
        link(last)
        link(v.tensor_copy(idxf[:, :, :].rearrange("p n e -> p (n e)"), idx[:, :, :].rearrange("p n e -> p (n e)")))
        dve.wait_ge(f_exp, 1)
        link(v.tensor_scalar(small[:, 2, :], small[:, 1, :], 1.0, None, ALU.add))
        link(v.reciprocal(small[:, 2, :], small[:, 2, :]))
        link(v.tensor_tensor(small[:, 3, :], small[:, 1, :], small[:, 2, :], ALU.mult))
        io = iota.rearrange("p (a e) -> p a e", a=1).to_broadcast([P, TT_N, EXPERTS])
        for j in range(2):
            link(v.tensor_tensor(hot[:, j, :, :], io, idxf[:, :, j:j + 1].to_broadcast([P, TT_N, EXPERTS]), ALU.is_equal))
            link(v.tensor_tensor(hot[:, j, :, :], hot[:, j, :, :], small[:, 2 + j, :].rearrange("p (n a) -> p n a", a=1).to_broadcast([P, TT_N, EXPERTS]),
                                 ALU.mult))
        link(v.tensor_tensor(comb[:, :, 1:WAYS], hot[:, 0, :, :], hot[:, 1, :, :], ALU.add))
        link(v.memset(comb[:, :, 0:1], 1.0))

        def gated(e, n):
            job = e * TT_N + n
            for half in range(2):
                dve.wait_ge(f_silu, 2 * job + half + 1)
                dve.wait_ge(f_gu_mm, 4 * job + 2 * half + 2)
                if half == 0 and not (isinstance(e, int) and job < 2):
                    if some(2 * job - 2):
                        dve.wait_ge(f_at_mm, 2 * job - 2)
                v.tensor_tensor(av[:, n % 2, half * FFH:(half + 1) * FFH], sg[:, half, :], gu[2 * half + 1][:, 0:FFH],
                                ALU.mult).then_inc(f_act, 1)

        def add(e, n):
            job = e * TT_N + n
            dve.wait_ge(f_dn_mm, job + 1)
            if not isinstance(e, int) or e > 0:
                if some(job - TT_N + 1):
                    dve.wait_ge(f_add, job - TT_N + 1)
            c = comb[:, n, e:e + 1] if isinstance(e, int) else comb[:, n, bass.ds(e, 1)]
            v.scalar_tensor_tensor(out=acc[:, n, :], in0=dn[n % 2][:, 0:HID], scalar=c, in1=acc[:, n, :], op0=ALU.mult,
                                   op1=ALU.add).then_inc(f_add, 1)

        def one_set(e):
            for n in range(TT_N):
                if n < TT_N - 1:
                    gated(e, n + 1)
                elif not isinstance(e, int) or e < WAYS - 1:
                    gated(e + 1, 0)
                add(e, n)

        gated(0, 0)
        one_set(0)
        with dve.Fori(1, WAYS - 1) as e:
            one_set(e)
        one_set(WAYS - 1)

    return {"sync": sync_program, "pe": tensor_program, "act": scalar_program, "dve": vector_program}


def build(nc, dram):
    with ExitStack() as ctx:
        t = {}
        t["sem"] = lambda name: ctx.enter_context(nc.semaphore(name))
        t["banks"] = [ctx.enter_context(nc.psum_tensor(f"bank{i}", [P, 512], F32)) for i in range(8)]
        keep = lambda name, shape, dt=F32: ctx.enter_context(nc.sbuf_tensor(name, shape, dt))
        t["acc"] = keep("acc", [P, TT_N, HID])
        t["thr"] = keep("thr", [P, TT_N])
        with ExitStack() as first:
            t["sb"] = lambda name, shape, dt=F32: first.enter_context(nc.sbuf_tensor(name, shape, dt))
            one = attention(nc, first, t, dram)
        t["sb"] = keep
        two = feed_forward(nc, t, dram)
        block = ctx.enter_context(nc.Block())

        @block.sync
        def _(sp):
            one["sync"](sp)
            two["sync"](sp)

        @block.tensor
        def _(pe):
            one["pe"](pe)
            two["pe"](pe)

        @block.scalar
        def _(act):
            one["act"](act)
            two["act"](act)

        @block.vector
        def _(dve):
            one["dve"](dve)
            two["dve"](dve)

        @block.gpsimd
        def _(pool):
            one["pool"](pool)


NAMES = {"x": "x", "ctx": "ctx_512", "Wcq": "L0_xattn_Wq", "Wck": "L0_xattn_Wk", "gamma": "L0_xattn_gamma_raw",
         "Wq": "L0_attn_Wq", "Wk": "L0_attn_Wk", "Wv": "L0_attn_Wv", "Wb": "L0_attn_Wb", "Wa": "L0_attn_Wa",
         "A_log": "L0_attn_A_log", "dt_bias": "L0_attn_dt_bias", "cq": "L0_attn_conv_q_w", "ck": "L0_attn_conv_k_w",
         "cv": "L0_attn_conv_v_w", "Wg": "L0_attn_Wg", "norm_w": "L0_attn_norm_w", "Wo": "L0_attn_Wo",
         "gate_w": "L0_ffn_gate_w", "base_gu": "L0_ffn_base_gate_up", "base_dn": "L0_ffn_base_down",
         "exp_gu": "L0_ffn_expert_gate_up", "exp_dn": "L0_ffn_expert_down"}


def kernel(**inputs):
    import numpy as _np
    import concourse.bacc as _bacc
    from concourse import mybir as _mybir
    from concourse.bass_utils import run_bass_kernel_spmd as _run

    nc = _bacc.Bacc("TRN2", target_bir_lowering=False, num_devices=1)
    arrays, dram = {}, {}
    for short, name in NAMES.items():
        a = _np.ascontiguousarray(inputs[name])
        if a.ndim == 0:
            a = a.reshape(1)
        arrays[f"in_{short}"] = a
        dram[short] = nc.dram_tensor(f"in_{short}", a.shape, _mybir.dt.from_np(a.dtype), kind="ExternalInput").ap()
    table = _np.concatenate([MASKS[k] for k in MASKS], axis=1)
    arrays["in_masks"] = table
    dram["masks"] = nc.dram_tensor("in_masks", table.shape, F32, kind="ExternalInput").ap()
    dram["sim"] = nc.dram_tensor("similarities", (TT_N, P, SEQ), F32, kind="Internal").ap()
    dram["out"] = nc.dram_tensor("out_0", (BATCH, SEQ, HID), F32, kind="ExternalOutput").ap()
    build(nc, dram)
    r = _run(nc, [arrays], core_ids=[0])
    return r.results[0]["out_0"]
```

```python
from contextlib import ExitStack

import numpy as np

import concourse.bass as bass
from concourse import mybir

F32 = mybir.dt.float32
ALU = mybir.AluOpType
ACT = mybir.ActivationFunctionType

P = 128
BATCH, SEQ, HID = 4, 256, 256
T = BATCH * SEQ
KT_H = HID // P
TT_N = T // P
HEADS, DH = 8, 128
STEPS = 64
CH = SEQ // STEPS
MU = 2 * STEPS
BC = BATCH * CH
LEVELS = 6
CONV = 4
EPS = 1e-5
CTX = 64
TOPK = int(SEQ * 0.3)
ROUNDS = -(-TOPK // 8)
LN_EXP = "natural_log_exp_and_others"
K_PROJ = 10
B_ITEMS = 20 + 12 * (LEVELS - 1) + 8


EXPERTS = 8
JOBS = 2 * T // P + EXPERTS - 1
SLOT_TILES = JOBS + JOBS % 2


def mask_table():
    j = np.arange(P)[:, None]
    i = np.arange(P)[None, :]
    out = {"ident": (i == j), "ones": np.ones((P, P)), "strict": (i > j)}
    t = np.arange(P)[:, None]
    out["cum"] = (t <= i // 2) & (t < STEPS)
    out["rest"] = (t > i // 2) & (t < STEPS)
    out["even"] = i == 2 * t
    out["odd"] = i == 2 * t + 1
    tt = np.arange(STEPS)[None, :]
    out["upto"] = t <= tt
    out["seen"] = t // 2 <= tt
    out["neg0t"] = (i == j).astype(float) - ((j % 2 == 0) & (i == j + 1))
    for lv in range(1, LEVELS + 1):
        s = 2 ** lv
        rows, cols = j, i
        off = (rows // (2 * s) == cols // (2 * s)) & ((rows // s) % 2 == 1) & ((cols // s) % 2 == 0)
        out[f"neg{lv}"] = (i == j).astype(float) - off
    c = np.zeros((P, 16))
    c[:, 3] = EPS
    c[:, 4] = 1.0
    c[:, 5] = -0.5
    c[:, 6] = 0.5
    c[:, 8:] = np.arange(8)
    out["scal"] = c
    out["tiles"] = np.broadcast_to(np.arange(SLOT_TILES), (P, SLOT_TILES))
    out["filled"] = np.broadcast_to(P * np.arange(TT_N), (P, TT_N))
    return {k: v.astype(np.float32) for k, v in out.items()}


MASKS = mask_table()
MASK_AT = {}
_at = 0
for _name, _m in MASKS.items():
    MASK_AT[_name] = (_at, _m.shape[1])
    _at += _m.shape[1]
MASK_W = _at


def some(v):
    return not isinstance(v, int) or v > 0


class Head:

    def __init__(self, h, par, use):
        self.h, self.par, self.use = h, par, use


def run_heads(eng, step):
    head = lambda h: Head(h, h % 2, h // 2) if 0 <= h < HEADS else None
    for s in range(4):
        step(head(s), head(s - 1), head(s - 2), head(s - 3))
    with eng.Fori(0, HEADS // 2 - 2) as m:
        step(Head(2 * m + 4, 0, m + 2), Head(2 * m + 3, 1, m + 1), Head(2 * m + 2, 0, m + 1), Head(2 * m + 1, 1, m))
        step(Head(2 * m + 5, 1, m + 2), Head(2 * m + 4, 0, m + 2), Head(2 * m + 3, 1, m + 1), Head(2 * m + 2, 0, m + 1))
    for s in range(HEADS, HEADS + 3):
        step(None, head(s - 1), head(s - 2), head(s - 3))


def b_items():
    out = []
    for b in range(BATCH):
        out += [("gram", b), ("qk", b), ("vtok", b)]
    out += [("x1", b) for b in range(BATCH)]
    for lv in range(1, LEVELS + 1):
        out += [("p", (lv - 1) * BATCH + b) for b in range(BATCH)]
        out += [("xt", (lv - 1) * BATCH + b) for b in range(BATCH)]
        if lv < LEVELS:
            out += [("x", (lv - 1) * BATCH + b) for b in range(BATCH)]
    out += [("kend", b) for b in range(BATCH)]
    assert len(out) == B_ITEMS
    return out


ITEMS = b_items()
QK_END = max(i for i, (kind, _) in enumerate(ITEMS) if kind == "qk") + 1
V_END = max(i for i, (kind, _) in enumerate(ITEMS) if kind == "vtok") + 1
PRE = 4 * BATCH
PER_HEAD = {k: sum(1 for kind, _ in ITEMS if kind == k) for k in ("gram", "qk", "kend", "vtok", "x1", "p", "x", "xt")}


def attention(nc, ctx, t, dram):
    sb, sem = t["sb"], t["sem"]

    masks = sb("masks", [P, MASK_W])

    def mask(name, rows=P):
        at, n = MASK_AT[name]
        return masks[0:rows, at:at + n]

    ident, ones = mask("ident"), mask("ones")
    eps, one = (mask("scal")[:, i:i + 1] for i in (3, 4))
    minus_half, half = (mask("scal")[:, i:i + 1] for i in (5, 6))
    acc = t["acc"]
    stats = sb("stats", [P, TT_N, 6])
    mv = sb("mv", [P, TT_N, 2])
    lnv = sb("lnv", [P, TT_N])
    rstd = sb("rstd", [P, TT_N])
    xnT = sb("xnT", [P, KT_H, T])
    wab = sb("wab", [P, KT_H, 24])
    rows = sb("rows", [STEPS, 2, HEADS])
    eA = sb("eA", [STEPS, HEADS])
    g_sb = sb("g_sb", [STEPS, HEADS, BC])
    beta_sb = sb("beta_sb", [STEPS, 2, HEADS, BC])
    scal = sb("scal", [P, HEADS, 4, BC])
    cw = sb("cw", [P, HEADS, 5, CONV])
    normw = sb("normw", [P, 1])
    wbuf = [sb(f"wbuf{i}", [P, KT_H, 5, DH]) for i in range(2)]
    wo = [sb(f"wo{i}", [P, HID]) for i in range(2)]
    wg = [sb(f"wg{i}", [P, KT_H, DH]) for i in range(2)]
    cwh = [sb(f"cwh{i}", [P, 5, CONV]) for i in range(2)]
    sh = [sb(f"sh{i}", [P, 4, BC]) for i in range(2)]
    kT = [sb(f"kT{i}", [P, BATCH, CH, MU]) for i in range(2)]
    qE = [sb(f"qE{i}", [P, BATCH, CH, STEPS]) for i in range(2)]

    vtok = [sb(f"vtok{i}", [P, BATCH, CH, DH]) for i in range(2)]
    mq = [sb(f"mq{i}", [P, BATCH, CH, STEPS]) for i in range(2)]
    gate = [sb(f"gate{i}", [P, T]) for i in range(2)]
    y = [sb(f"y{i}", [P, 2, SEQ]) for i in range(2)]
    kraw = sb("kraw", [P, 2 * T])
    qraw = sb("qraw", [P, T])
    vraw = sb("vraw", [P, 2 * T])
    ksum = sb("ksum", [P, BC])
    kn = sb("kn", [P, BC])
    beta_n = sb("beta_n", [P, BC])
    qn = sb("qn", [P, HEADS, TT_N])
    factor = sb("factor", [P, TT_N])
    kend = sb("kend", [P, BATCH, CH, DH])
    osq = sb("osq", [P, T])
    sq = [osq[:, i * 512:(i + 1) * 512] for i in range(2)]
    gm = sb("gm", [STEPS, BC, STEPS])
    dx = sb("dx", [P, BC, STEPS])
    ex = sb("ex", [P, BC, STEPS])
    dm = sb("dm", [P, BC, STEPS])
    aT = sb("aT", [P, BATCH, CH, MU])
    X = sb("X", [P, BATCH, CH, MU])
    XT = sb("XT", [P, BATCH, CH, MU])
    Pn = sb("Pn", [P, BATCH, CH, MU])
    TT = sb("TT", [P, BATCH, CH, MU])
    R = sb("R", [P, BATCH, DH])
    U = sb("U", [P, BATCH, DH])
    S = sb("S", [P, BATCH, DH])
    oT = sb("oT", [P, BATCH, SEQ])
    og = oT[:, :, :].rearrange("p b t -> p (b t)")

    bankA, bankB, bankC = t["banks"][0:2], t["banks"][2:6], t["banks"][6:8]

    zs = vraw[0:STEPS, 0:BC * 24].rearrange("p (n c) -> p n c", c=24)
    zt = vraw[0:STEPS, 512:512 + 768].rearrange("p (i n) -> p i n", i=3)
    flat = [w[:, :, :, :].rearrange("p b c n -> p (b c n)") for w in (X, XT, Pn)]
    hT, kcT = flat[0][0:CTX, 0:T], flat[0][0:CTX, T:2 * T]
    qcT, ctok = flat[1][0:CTX, 0:T], flat[1][:, T:T + 512]
    wqk, wqkT = flat[1][0:CTX, T + 512:T + 640], flat[1][0:CTX, T + 640:T + 768]
    simout = flat[2]
    simw = [sb(f"simw{i}", [P, SEQ]) for i in range(2)]
    m8 = sb("m8", [P, 8])
    thr = t["thr"]
    zero = oT[:, 0, :]
    zero_done, slots_zeroed = sem("zero_done"), sem("slots_zeroed")
    t["slots_zeroed"] = slots_zeroed
    xn = kraw[:, :].rearrange("p (n d) -> p n d", n=TT_N)

    masks_in = sem("masks_in")
    x_in = sem("x_in")
    small_in = sem("small_in")
    stats_done = sem("stats_done")
    mv_done = sem("mv_done")
    lnv_done = sem("lnv_done")
    rstd_done = sem("rstd_done")
    xn_done = sem("xn_done")
    xnt_mm = sem("xnt_mm")
    xnt_done = sem("xnt_done")
    z_mm = sem("z_mm")
    z_done = sem("z_done")
    ctx_in = sem("ctx_in")
    ctx_mm = sem("ctx_mm")
    ctx_used = sem("ctx_used")
    sim_out = sem("sim_out")
    sim_in0 = sem("sim_in0")
    sim_in1 = sem("sim_in1")
    topk_step = sem("topk_step")
    sp_step = sem("sp_step")
    g_done = sem("g_done")
    beta_done = sem("beta_done")
    scal_mm = sem("scal_mm")
    scal_done = sem("scal_done")
    pre_free = sem("pre_free")
    w_in0 = sem("w_in0")
    w_in1 = sem("w_in1")
    wo_in0 = sem("wo_in0")
    wo_in1 = sem("wo_in1")
    cwh_done = sem("cwh_done")
    sh_done = sem("sh_done")
    proj_done = sem("proj_done")
    gate_mm = sem("gate_mm")
    evac_done = sem("evac_done")
    conv_step = sem("conv_step")
    silu_done = sem("silu_done")
    gate_done = sem("gate_done")
    gm_done = sem("gm_done")
    dmat_done = sem("dmat_done")
    dexp_done = sem("dexp_done")
    dm_done = sem("dm_done")
    sq_done = sem("sq_done")
    norm_mm = sem("norm_mm")
    sums_done = sem("sums_done")
    beta_step = sem("beta_step")
    kn_done = sem("kn_done")
    osums_done = sem("osums_done")
    factor_done = sem("factor_done")
    qe_done = sem("qe_done")
    b_mm = sem("b_mm")
    at_done = sem("at_done")
    diag0 = sem("diag0")
    diag1 = sem("diag1")
    gram_used = sem("gram_used")
    qk_used = sem("qk_used")
    kend_done = sem("kend_done")
    vtok_done = sem("vtok_done")
    x1_used = sem("x1_used")
    p_used = sem("p_used")
    x_used = sem("x_used")
    xt_used = sem("xt_used")
    ks_mm = sem("ks_mm")
    r_done = sem("r_done")
    u_mm = sem("u_mm")
    u_done = sem("u_done")
    o_mm = sem("o_mm")
    o_done = sem("o_done")
    s_mm = sem("s_mm")
    s_done = sem("s_done")
    osq_done = sem("osq_done")
    oss_mm = sem("oss_mm")
    kt_copied = sem("kt_copied")
    og_step = sem("og_step")
    wo_mm = sem("wo_mm")
    acc_done = sem("acc_done")
    t["acc_done"] = acc_done
    sim_in = [sim_in0, sim_in1]
    w_in = [w_in0, w_in1]
    wo_in = [wo_in0, wo_in1]

    raised = {"pe": [o_mm, oss_mm, u_mm, wo_mm], "dve": [acc_done, og_step], "act": [osq_done]}

    def raise_once(eng, who):
        for n in raised[who]:
            eng.sem_inc(n, 1)

    left = {"gram": at_done, "qk": qk_used, "kend": kend_done, "vtok": vtok_done, "x1": x1_used,
            "p": p_used, "x": x_used, "xt": xt_used}

    def a_free(pe, kind, i, h):
        if kind == "decay":
            if i < 2:
                if some(h):
                    pe.wait_ge(sums_done, 6 * h - 1 + i)
            else:
                pe.wait_ge(dexp_done, 4 * h + i - 1)
        elif kind == "proj":
            if i < 2:
                pe.wait_ge(dexp_done, 4 * h + 3 + i)
            elif i < 7:
                pe.wait_ge(conv_step, 30 * h + 3 * i - 3)
            else:
                pe.wait_ge(conv_step, 30 * h + 3 * i)
        elif kind == "norm":
            if i == 0:
                pe.wait_ge(conv_step, 30 * h + 18)
            elif i < 4:
                pe.wait_ge(sums_done, 6 * h + i)
            elif some(h):
                pe.wait_ge(gate_done, 2 * h - 5 + i)
            elif i == 4:
                pe.wait_ge(conv_step, 30 * h + 30)
            else:
                pe.wait_ge(sums_done, 6 * h + 4)
        elif isinstance(h, int) and h == HEADS - 1:
            pe.wait_ge(sums_done, 6 * HEADS - 1 + i)
        elif i == 0:
            pe.wait_ge(conv_step, 30 * (h + 1) + 30)
        else:
            pe.wait_ge(sums_done, 6 * (h + 1) + 4)

    proj_bank = lambda p: p % 2 if p < 6 else 0
    norm_bank = lambda i: 1 if i < 4 else i % 2

    def b_free(pe, idx, h):
        if idx >= 4:
            kind, k = ITEMS[idx - 4]
            pe.wait_ge(left[kind], PER_HEAD[kind] * h + k + 1)
        elif not isinstance(h, int) or h > 0:
            kind, k = ITEMS[idx - 4 + B_ITEMS]
            pe.wait_ge(left[kind], PER_HEAD[kind] * (h - 1) + k + 1)

    def diag(which, eng, B, b):
        mine, k = (diag0, b) if b < BATCH // 2 else (diag1, b - BATCH // 2)
        eng.wait_ge(at_done, 4 * B.h + b + 1)
        which.tensor_tensor(aT[:, b, :, :], aT[:, b, :, :], mask("strict").rearrange("p (a n) -> p a n", a=1).to_broadcast([P, CH, MU]),
                            ALU.mult).then_inc(mine, 1)
        eng.wait_ge(mine, 6 * B.h + 3 * k + 1)
        which.tensor_tensor(aT[:, b, :, :], aT[:, b, :, :], ident.rearrange("p (a n) -> p a n", a=1).to_broadcast([P, CH, MU]),
                            ALU.add).then_inc(mine, 1)
        eng.wait_ge(mine, 6 * B.h + 3 * k + 2)
        if not isinstance(B.h, int) or B.h > 0:
            eng.wait_ge(b_mm, B_ITEMS * B.h)
        else:
            eng.wait_ge(sim_out, 64)
        which.tensor_tensor(XT[:, b, :, :], aT[:, b, :, :], mask("neg0t").rearrange("p (a n) -> p a n", a=1).to_broadcast([P, CH, MU]),
                            ALU.mult).then_inc(mine, 1)

    def sync_program(sp):
        sp.dma_start(ctok.rearrange("p (n d) -> p n d", d=CTX),
                     dram["ctx"].rearrange("b s d -> (b s) d").rearrange("(n p) d -> p n d", p=P)).then_inc(ctx_in, 16)
        sp.dma_start(wqk[:, 0:CTX], dram["Wcq"]).then_inc(ctx_in, 16)
        sp.dma_start(wqk[:, CTX:2 * CTX], dram["Wck"]).then_inc(ctx_in, 16)
        sp.dma_start(masks[:, :], dram["masks"]).then_inc(masks_in, 16)
        sp.dma_start(acc[:, :, :], dram["x"].rearrange("b s d -> (b s) d").rearrange("(n p) d -> p n d", p=P)).then_inc(x_in, 16)
        sp.dma_start(wab[:, :, 0:16], dram["Wb"].rearrange("(k p) n -> p k n", p=P)).then_inc(small_in, 16)
        sp.dma_start(wab[:, :, 16:24], dram["Wa"].rearrange("(k p) n -> p k n", p=P)).then_inc(small_in, 16)
        sp.dma_start(rows[:, 0, :], dram["A_log"].rearrange("(a n) -> a n", a=1).to_broadcast([STEPS, HEADS])).then_inc(small_in, 16)
        sp.dma_start(rows[:, 1, :], dram["dt_bias"].rearrange("(a n) -> a n", a=1).to_broadcast([STEPS, HEADS])).then_inc(small_in, 16)
        for i, (w, j) in enumerate((("cq", 0), ("ck", 0), ("ck", 1), ("cv", 0), ("cv", 1))):
            src = dram[w].rearrange("(j h p) a k -> j p h (a k)", p=P, h=HEADS)[j]
            sp.dma_start(cw[:, :, i, :], src).then_inc(small_in, 16)
        sp.dma_start(normw[:, :], dram["norm_w"].rearrange("(p a) -> p a", a=1)).then_inc(small_in, 16)

        for i in range(4):
            if some(8 + i):
                sp.wait_ge(ctx_used, 8 + i)
            sp.dma_start(dram["sim"][2 * i:2 * i + 2].rearrange("n p m -> p n m"),
                         simout[:, i * 512:(i + 1) * 512].rearrange("p (n m) -> p n m", n=2)).then_inc(sim_out, 16)
        sp.wait_ge(sim_out, 64)

        def step(A, B, C, E):
            if A:
                if not isinstance(A.h, int) or A.h >= 2:
                    if some(2 * ROUNDS * (A.h - 1)):
                        sp.wait_ge(topk_step, 2 * ROUNDS * (A.h - 1))
                sp.dma_start(simw[A.par][:, :], dram["sim"][A.h]).then_inc(sim_in[A.par], 16)
                if not isinstance(A.h, int) or A.h >= 2:
                    if some(K_PROJ * (A.h - 1)):
                        sp.wait_ge(proj_done, K_PROJ * (A.h - 1))
                for i, (w, j) in enumerate((("Wq", 0), ("Wk", 0), ("Wk", 1), ("Wv", 0), ("Wv", 1))):
                    src = dram[w].rearrange("(k p) (j h n) -> p k j h n", p=P, n=DH, h=HEADS)[:, :, j, A.h, :]
                    sp.dma_start(wbuf[A.par][:, :, i, :], src).then_inc(w_in[A.par], 16)
            if B:
                if not isinstance(B.h, int) or B.h >= 2:
                    if some(4 * (B.h - 1)):
                        sp.wait_ge(wo_mm, 4 * (B.h - 1) + 1)
                sp.dma_start(wg[B.par][:, :, :], dram["Wg"].rearrange("(k p) (h n) -> h p k n", p=P, n=DH)[B.h]).then_inc(wo_in[B.par], 16)
                sp.dma_start(wo[B.par][:, :], dram["Wo"].rearrange("(h p) n -> h p n", p=P)[B.h]).then_inc(wo_in[B.par], 16)
            if B and isinstance(B.h, int) and B.h == 0:
                sp.wait_ge(zero_done, 1)
                for m in range(SLOT_TILES):
                    sp.dma_start(dram["slots_x"][m], zero).then_inc(slots_zeroed, 16)

        run_heads(sp, step)

    PROJ = [1, 2, 0, 3, 4]

    def context_products(pe):
        mm = nc.tensor.matmul
        pe.wait_ge(ctx_in, 48)
        for i in range(11):
            bank = bankC[i % 2]
            if some(i - 1):
                pe.wait_ge(ctx_used, i - 1)
            if i < 2:
                for k in range(4):
                    last = nc.tensor.transpose(bank[0:CTX, k * P:(k + 1) * P], ctok[:, (4 * i + k) * CTX:(4 * i + k + 1) * CTX], ident)
            elif i == 2:
                for k in range(2):
                    last = nc.tensor.transpose(bank[0:CTX, k * CTX:(k + 1) * CTX], wqk[:, k * CTX:(k + 1) * CTX], ident[0:CTX, 0:CTX])
            elif i < 7:
                pe.wait_ge(ctx_used, 3)
                w, half = (i - 3) // 2, (i - 3) % 2
                last = mm(bank[0:CTX, :], wqkT[:, w * CTX:(w + 1) * CTX], hT[:, half * 512:(half + 1) * 512], start=True, stop=True)
            else:
                pe.wait_ge(ctx_used, 7)
                for k in range(2):
                    n = 2 * (i - 7) + k
                    last = mm(bank[:, k * SEQ:(k + 1) * SEQ], qcT[:, n * P:(n + 1) * P],
                              kcT[:, n // 2 * SEQ:(n // 2 + 1) * SEQ], start=True, stop=True)
            last.then_inc(ctx_mm, 1)

    def context_copies(act):
        dst = [hT[:, 0:512], hT[:, 512:T], wqkT, qcT[:, 0:512], qcT[:, 512:T], kcT[:, 0:512], kcT[:, 512:T]] \
            + [simout[:, i * 512:(i + 1) * 512] for i in range(4)]
        for i, d in enumerate(dst):
            act.wait_ge(ctx_mm, i + 1)
            rows_, cols = d.shape[0], d.shape[1]
            nc.scalar.activation(d, bankC[i % 2][0:rows_, 0:cols], ACT.Copy).then_inc(ctx_used, 1)

    def tensor_program(pe):
        mm = nc.tensor.matmul
        raise_once(pe, "pe")
        pe.wait_ge(masks_in, 16)
        context_products(pe)
        for n in range(4):
            pe.wait_ge(xn_done, 2 * n + 2)
            for k in range(4):
                tile, kt = 2 * n + k // 2, k % 2
                last = nc.tensor.transpose(bankB[n][:, k * P:(k + 1) * P], xn[:, tile, kt * P:(kt + 1) * P], ident)
            last.then_inc(xnt_mm, 1)
        pe.wait_ge(small_in, 16 * 10)
        pe.wait_ge(xnt_done, 4)
        for bc in range(BC):
            for kt in range(KT_H):
                last = mm(bankA[0][0:STEPS, bc * 24:(bc + 1) * 24], xnT[:, kt, bc * STEPS:(bc + 1) * STEPS], wab[:, kt, :],
                          start=kt == 0, stop=kt == 1)
        last.then_inc(z_mm, 1)
        pe.wait_ge(g_done, 1)
        pe.wait_ge(beta_done, 1)
        gf = g_sb[:, :, :].rearrange("p h n -> p (h n)")
        for i, m in enumerate(("cum", "rest", "ones")):
            mm(bankA[1][:, i * P:(i + 1) * P], mask(m, STEPS), gf, start=True, stop=True)
        for i, m in enumerate(("even", "odd")):
            last = mm(bankA[1][:, 3 * P:4 * P], mask(m, STEPS), beta_sb[:, i, :, :].rearrange("p h n -> p (h n)"),
                      start=i == 0, stop=i == 1)
        last.then_inc(scal_mm, 1)
        pe.wait_ge(scal_done, 4)

        def proj(A, p):
            wblk = PROJ[p // 2]
            if p == 0:
                pe.wait_ge(w_in[A.par], 5 * 16 * (A.use + 1))
            a_free(pe, "proj", p, A.h)
            for kt in range(KT_H):
                last = mm(bankA[proj_bank(p)][:, :], wbuf[A.par][:, kt, wblk, :], xnT[:, kt, (p % 2) * 512:(p % 2 + 1) * 512],
                          start=kt == 0, stop=kt == 1)
            last.then_inc(proj_done, 1)

        def gates(B):
            pe.wait_ge(wo_in[B.par], 32 * (B.use + 1))
            for i in range(2):
                a_free(pe, "gate", i, B.h)
                for kt in range(KT_H):
                    last = mm(bankA[i][:, :], wg[B.par][:, kt, :], xnT[:, kt, i * 512:(i + 1) * 512], start=kt == 0, stop=kt == 1)
                last.then_inc(gate_mm, 1)

        def decays(A, these):
            pe.wait_ge(gm_done, A.h + 1)
            for i in these:
                a_free(pe, "decay", i, A.h)
                mm(bankA[i % 2][:, :], mask("rest" if i < 2 else "ones", STEPS),
                   gm[:, (i % 2) * 8:(i % 2 + 1) * 8, :].rearrange("p n t -> p (n t)"),
                   start=True, stop=True).then_inc(dmat_done, 1)

        def norm(A, i):
            pe.wait_ge(sq_done, 6 * A.h + i + 1)
            a_free(pe, "norm", i, A.h)
            for c in range(4):
                last = mm(bankA[norm_bank(i)][:, c:c + 1], sq[i % 2][:, c * P:(c + 1) * P], ones[:, 0:1], start=True, stop=True)
            last.then_inc(norm_mm, 1)

        def b_item(idx, B):
            kind, n = ITEMS[idx]
            b, lv = n % BATCH, n // BATCH + 1
            h, par, bank = B.h, B.par, bankB[idx % 4]
            b_free(pe, idx, h)
            if kind == "gram" and b == 0:
                pe.wait_ge(silu_done, 10 * h + 10)
            if kind == "kend" and b == 0:
                pe.wait_ge(kt_copied, 4 * h + 4)
            if kind == "vtok" and b == 0:
                pe.wait_ge(silu_done, 10 * h + 10)
            if kind == "x1":
                pe.wait_ge(diag0 if b < 2 else diag1, 6 * h + 3 * (b % 2) + 3)
            if kind == "p":
                if lv == 1:
                    pe.wait_ge(diag0 if b < 2 else diag1, 6 * h + 3 * (b % 2) + 3)
                    pe.wait_ge(x1_used, 4 * h + b + 1)
                else:
                    pe.wait_ge(x_used, 20 * h + (lv - 2) * BATCH + b + 1)
            if kind == "x":
                pe.wait_ge(xt_used, 24 * h + n + 1)
            if kind == "xt":
                pe.wait_ge(p_used, 24 * h + n + 1)
                if lv > 1:
                    if some(24 * h + n - BATCH + 1):
                        pe.wait_ge(xt_used, 24 * h + n - BATCH + 1)
            for c in range(CH):
                out = bank[:, c * P:(c + 1) * P]
                kc = kraw[:, (b * CH + c) * MU:(b * CH + c + 1) * MU]
                if kind == "gram":
                    last = mm(out, kc, kc, start=True, stop=True)
                elif kind == "qk":
                    at = (b * CH + c) * STEPS
                    last = mm(bank[:, c * STEPS:(c + 1) * STEPS], kc, qraw[:, at:at + STEPS], start=True, stop=True)
                elif kind == "kend":
                    last = nc.tensor.transpose(out, kT[par][:, b, c, :], ident)
                elif kind == "vtok":
                    at = (b * CH + c) * MU
                    last = nc.tensor.transpose(out, vraw[:, at:at + MU], ident)
                elif kind in ("x1", "x"):
                    last = nc.tensor.transpose(out, XT[:, b, c, :], ident)
                elif kind == "p":
                    last = mm(out, aT[:, b, c, :], X[:, b, c, :], start=True, stop=True)
                else:
                    last = mm(out, Pn[:, b, c, :], XT[:, b, c, :], start=True, stop=True)
            last.then_inc(b_mm, 1)

        def scan(C, slot):
            c, ph = slot // 3, slot % 3
            h, par = C.h, C.par
            if ph == 0 and c > 0:
                for b in range(BATCH):
                    if some(12 * h + 4 * c):
                        pe.wait_ge(s_done, 12 * h + 4 * c)
                    last = mm(bankC[0][:, b * P:(b + 1) * P], kT[par][:, b, c, :], S[:, b, :], start=True, stop=True)
                last.then_inc(ks_mm, 1)
            if ph == 1:
                if c > 0:
                    if some(4 * h + c):
                        pe.wait_ge(o_done, 4 * h + c)
                elif not isinstance(h, int) or h > 0:
                    if some(4 * h):
                        pe.wait_ge(acc_done, 4 * h + 1)
                if c == 0:
                    pe.wait_ge(xt_used, 24 * h + 24)
                for b in range(BATCH):
                    if c > 0:
                        pe.wait_ge(r_done, 12 * h + 4 * (c - 1) + b + 1)
                    last = mm(bankC[1][:, b * P:(b + 1) * P], TT[:, b, c, :], R[:, b, :] if c else vtok[par][:, b, c, :],
                              start=True, stop=True)
                last.then_inc(u_mm, 1)
            if ph == 2:
                pe.wait_ge(u_done, 4 * h + c + 1)
                if c == 0:
                    pe.wait_ge(qe_done, 2 * h + 2)
                for b in range(BATCH):
                    out = bankC[1][:, b * STEPS:(b + 1) * STEPS]
                    if c > 0:
                        mm(out, S[:, b, :], qE[par][:, b, c, :], start=True, stop=False)
                    last = mm(out, U[:, b, :], mq[par][:, b, c, :], start=c == 0, stop=True)
                last.then_inc(o_mm, 1)
                if c < CH - 1:
                    for b in range(BATCH):
                        last = mm(bankC[0][:, b * P:(b + 1) * P], kend[:, b, c, :], U[:, b, :], start=True, stop=True)
                    last.then_inc(s_mm, 1)

        def out_sums(C):
            pe.wait_ge(o_done, 4 * C.h + 4)
            pe.wait_ge(osq_done, C.h + 2)
            for n in range(TT_N):
                last = mm(bankC[0][:, n:n + 1], osq[:, n * P:(n + 1) * P], ones[:, 0:1], start=True, stop=True)
            last.then_inc(oss_mm, 1)

        def out_proj(C):
            pe.wait_ge(og_step, C.h + 2)
            pe.wait_ge(osums_done, C.h + 1)
            for n in range(4):
                if n >= 2:
                    if some(4 * C.h + n - 1):
                        pe.wait_ge(acc_done, 4 * C.h + n)
                for k in range(2):
                    tile = 2 * n + k
                    last = mm(bankC[n % 2][:, k * HID:(k + 1) * HID], og[:, tile * P:(tile + 1) * P], wo[C.par][:, :],
                              start=True, stop=True)
                last.then_inc(wo_mm, 1)

        def step(A, B, C, E):
            if B:
                for idx in range(PRE - BATCH):
                    b_item(idx, B)
            if E:
                out_sums(E)
            if A:
                decays(A, (0, 1))
            if B:
                for idx in range(PRE - BATCH, PRE):
                    b_item(idx, B)
            if E:
                out_proj(E)
            at = PRE
            for slot in range(12):
                if B:
                    for idx in range(at, at + BATCH):
                        b_item(idx, B)
                    at += BATCH
                if A and slot == 0:
                    decays(A, (2, 3))
                if C:
                    scan(C, slot)
                if B and slot % 2 and slot < 11:
                    for idx in range(at, at + BATCH):
                        b_item(idx, B)
                    at += BATCH
                if A and slot < 10:
                    proj(A, slot)
                if B and slot == 10:
                    gates(B)
                if A and slot >= 6:
                    norm(A, slot - 6)
            if B:
                for idx in range(at, B_ITEMS):
                    b_item(idx, B)

        run_heads(pe, step)

    def scalar_program(act):
        a = nc.scalar.activation
        raise_once(act, "act")
        act.wait_ge(masks_in, 16)
        context_copies(act)
        nc.scalar.preload_act_table_set(LN_EXP)
        act.wait_ge(mv_done, TT_N)
        a(lnv[:, :], mv[:, :, 1], ACT.Ln, bias=eps).then_inc(lnv_done, 1)
        act.wait_ge(lnv_done, 1)
        a(rstd[:, :], lnv[:, :], ACT.Exp, scale=-0.5).then_inc(rstd_done, 1)
        for n in range(4):
            act.wait_ge(xnt_mm, n + 1)
            a(xnT[:, :, 2 * n * P:(2 * n + 2) * P].rearrange("p k (m c) -> p m k c", m=2),
              bankB[n][:, :].rearrange("p (m k c) -> p m k c", m=2, k=2), ACT.Copy).then_inc(xnt_done, 1)
        act.wait_ge(z_mm, 1)
        act.wait_ge(small_in, 160)
        n1, n2 = BC * HEADS, BC * HEADS * 2
        a(zs[:, :, :], bankA[0][0:STEPS, 0:BC * 24].rearrange("p (n c) -> p n c", c=24), ACT.Copy).then_inc(sp_step, 1)
        act.wait_ge(sp_step, 3)
        a(zt[:, 1, 0:n1], zt[:, 1, 0:n1], ACT.Exp).then_inc(sp_step, 1)
        act.wait_ge(sp_step, 4)
        a(zt[:, 1, 0:n1], zt[:, 1, 0:n1], ACT.Ln, bias=one[0:STEPS]).then_inc(sp_step, 1)
        a(eA[:, :], rows[:, 0, :], ACT.Exp).then_inc(sp_step, 1)
        a(zt[:, 2, 0:n2].rearrange("p (n c) -> p n c", c=16), zs[:, :, 0:16], ACT.Exp, scale=-1.0).then_inc(sp_step, 1)
        act.wait_ge(scal_mm, 1)
        v = bankA[1][:, :].rearrange("p (i h n) -> p i h n", i=4, h=HEADS)
        for i, f in enumerate((ACT.Exp, ACT.Exp, ACT.Exp, ACT.Copy)):
            a(scal[:, :, i, :], v[:, i, :, :], f).then_inc(scal_done, 1)

        def evac(A, p):
            act.wait_ge(proj_done, K_PROJ * A.h + p + 1)
            if some(10 * A.h + p - 1):
                act.wait_ge(silu_done, 10 * A.h + p - 1)
            if p == 0:
                act.wait_ge(cwh_done, A.h + 1)
            cb = PROJ[p // 2]
            a(y[p % 2][:, :, :].rearrange("p b t -> p (b t)"), bankA[proj_bank(p)][:, :], ACT.Copy,
              scale=cwh[A.par][:, cb, 3:4]).then_inc(evac_done, 1)

        def silu(A, p):
            act.wait_ge(conv_step, 30 * A.h + 3 * p + 3)
            half = p % 2
            if p == 0 and some(A.h):
                act.wait_ge(sq_done, 6 * A.h)
                act.wait_ge(b_mm, B_ITEMS * (A.h - 1) + QK_END)
                act.wait_ge(kt_copied, 4 * A.h)
            if p == 4 and some(A.h):
                act.wait_ge(qe_done, 2 * A.h)
            if p == 6 and (not isinstance(A.h, int) or A.h > 0):
                if some(B_ITEMS * (A.h - 1) + V_END):
                    act.wait_ge(b_mm, B_ITEMS * (A.h - 1) + V_END)
            dst = {0: kraw, 1: kraw, 2: qraw, 3: vraw, 4: vraw}[p // 2]
            if p // 2 == 2:
                out = qraw[:, half * 512:(half + 1) * 512]
            else:
                out = dst[:, :].rearrange("p (t j) -> p t j", j=2)[:, half * 512:(half + 1) * 512, (0, 1, 0, 0, 1)[p // 2]]
            a(out, y[half][:, :, :].rearrange("p b t -> p (b t)"), ACT.Silu).then_inc(silu_done, 1)

        def gates(B):
            if isinstance(B.h, int) and B.h == 0:
                act.wait_ge(slots_zeroed, 16 * SLOT_TILES)
            for i in range(2):
                if some(2 * B.h + 1 + i):
                    act.wait_ge(gate_mm, 2 * B.h + 1 + i)
                if not isinstance(B.h, int) or B.h >= 2:
                    act.wait_ge(og_step, B.h)
                a(gate[B.par][:, i * 512:(i + 1) * 512], bankA[i][:, :], ACT.Silu).then_inc(gate_done, 1)

        def decays(A, these):
            nc.scalar.preload_act_table_set(LN_EXP)
            for i in these:
                act.wait_ge(dmat_done, 4 * A.h + i + 1)
                if i == 0:
                    if some(4 * A.h):
                        act.wait_ge(at_done, 4 * A.h)
                if i == 2:
                    if some(2 * A.h):
                        act.wait_ge(qe_done, 2 * A.h)
                dst = (dx if i < 2 else ex)[:, (i % 2) * 8:(i % 2 + 1) * 8, :]
                a(dst.rearrange("p n t -> p (n t)"), bankA[i % 2][:, :], ACT.Exp).then_inc(dexp_done, 1)

        def square(A, i):
            if i >= 2:
                act.wait_ge(norm_mm, 6 * A.h + i - 1)
            if i == 0 and (not isinstance(A.h, int) or A.h >= 2):
                act.wait_ge(oss_mm, A.h - 1)
            act.wait_ge(silu_done, 10 * A.h + (4 if i < 4 else 6))
            src = kraw[:, i * 512:(i + 1) * 512] if i < 4 else qraw[:, (i - 4) * 512:(i - 3) * 512]
            a(sq[i % 2], src, ACT.Square).then_inc(sq_done, 1)

        def out_square(C, head):
            act.wait_ge(o_done, 4 * C.h + 4)
            act.wait_ge(oss_mm, C.h + 1)
            act.wait_ge(norm_mm, 6 * head + 6)
            a(osq[:, :], oT[:, :, :].rearrange("p b t -> p (b t)"), ACT.Square).then_inc(osq_done, 1)

        def keep_k(B):
            for b in range(BATCH):
                if b == 0:
                    act.wait_ge(silu_done, 10 * B.h + 10)
                if b == 0 and (not isinstance(B.h, int) or B.h >= 2):
                    act.wait_ge(ks_mm, 3 * (B.h - 1))
                    act.wait_ge(b_mm, B_ITEMS * (B.h - 1))
                a(kT[B.par][:, b, :, :].rearrange("p c n -> p (c n)"), kraw[:, b * 512:(b + 1) * 512], ACT.Copy).then_inc(kt_copied, 1)

        def copy_b(idx, B):
            kind, n = ITEMS[idx]
            b, lv = n % BATCH, n // BATCH + 1
            if kind not in ("vtok", "x1", "x", "xt"):
                return
            act.wait_ge(b_mm, B_ITEMS * B.h + idx + 1)
            if kind == "x1" and b == 0:
                act.wait_ge(sim_out, 64)
            if kind == "vtok":
                if b == 0:
                    act.wait_ge(kn_done, B.h + 1)
                    if not isinstance(B.h, int) or B.h >= 2:
                        act.wait_ge(u_mm, 4 * (B.h - 1) + 1)
                for c in range(CH):
                    last = a(vtok[B.par][:, b, c, :], bankB[idx % 4][:, c * P:(c + 1) * P], ACT.Copy, scale=kn[:, b * CH + c:b * CH + c + 1])
                last.then_inc(vtok_done, 1)
                return
            dst = {"x1": X, "x": X, "xt": TT if lv == LEVELS else XT}[kind]
            a(dst[:, b, :, :].rearrange("p c n -> p (c n)"), bankB[idx % 4][:, :], ACT.Copy).then_inc(left[kind], 1)

        def scan(C, slot):
            c, ph = slot // 3, slot % 3
            if ph == 2:
                act.wait_ge(o_mm, 4 * C.h + c + 2)
                if c == 0:
                    act.wait_ge(og_step, C.h + 1)
                    act.wait_ge(osq_done, C.h + 1)
                a(oT[:, :, c * STEPS:(c + 1) * STEPS], bankC[1][:, 0:BATCH * STEPS].rearrange("p (b t) -> p b t", b=BATCH),
                  ACT.Copy).then_inc(o_done, 1)


        def step(A, B, C, E):
            if B:
                for idx in range(PRE - BATCH):
                    copy_b(idx, B)
            if A:
                decays(A, (0, 1))
            if B:
                keep_k(B)
                for idx in range(PRE - BATCH, PRE):
                    copy_b(idx, B)
            at = PRE
            for slot in range(12):
                if B:
                    for idx in range(at, at + BATCH):
                        copy_b(idx, B)
                    at += BATCH
                if A and slot == 0:
                    decays(A, (2, 3))
                if C:
                    scan(C, slot)
                if B and slot % 2 and slot < 11:
                    for idx in range(at, at + BATCH):
                        copy_b(idx, B)
                    at += BATCH
                if A and slot < 10:
                    evac(A, slot)
                if A and 1 <= slot <= 10:
                    silu(A, slot - 1)
                if B and slot == 10:
                    gates(B)
                if A and 5 <= slot <= 10:
                    square(A, slot - 5)
            if C:
                out_square(C, A.h if A else HEADS - 1)

        run_heads(act, step)

    def vector_program(dve):
        v = nc.vector
        raise_once(dve, "dve")
        dve.wait_ge(x_in, 16)
        for n in range(TT_N):
            v.bn_stats(stats[:, n, :], acc[:, n, :]).then_inc(stats_done, 1)
        for n in range(TT_N):
            dve.wait_ge(stats_done, n + 1)
            v.bn_aggr(mv[:, n, :], stats[:, n, :]).then_inc(mv_done, 1)
        dve.wait_ge(rstd_done, 1)
        for n in range(TT_N):
            v.tensor_scalar(xn[:, n, :], acc[:, n, :], mv[:, n, 0:1], rstd[:, n:n + 1], ALU.subtract, ALU.mult).then_inc(xn_done, 1)
        n1, n2 = BC * HEADS, BC * HEADS * 2
        dve.wait_ge(sp_step, 1)
        za = zt[:, 0, 0:n1].rearrange("p (n h) -> p n h", h=HEADS)
        v.tensor_tensor(za, zs[:, :, 16:24], rows[:, 1:2, :].to_broadcast([STEPS, BC, HEADS]), ALU.add).then_inc(sp_step, 1)
        dve.wait_ge(sp_step, 2)
        v.scalar_tensor_tensor(out=zt[:, 1, 0:n1], in0=zt[:, 0, 0:n1], scalar=-1.0, in1=zt[:, 0, 0:n1], op0=ALU.mult,
                               op1=ALU.min).then_inc(sp_step, 1)
        dve.wait_ge(sp_step, 7)
        v.scalar_tensor_tensor(out=zt[:, 0, 0:n1], in0=zt[:, 0, 0:n1], scalar=0.0, in1=zt[:, 1, 0:n1], op0=ALU.max,
                               op1=ALU.add).then_inc(sp_step, 1)
        dve.wait_ge(sp_step, 8)
        v.scalar_tensor_tensor(out=g_sb[:, :, :].rearrange("p h n -> p n h"), in0=za, scalar=-1.0,
                               in1=eA[:, :].rearrange("p (a h) -> p a h", a=1).to_broadcast([STEPS, BC, HEADS]), op0=ALU.mult,
                               op1=ALU.mult).then_inc(g_done, 1)
        v.tensor_scalar(zt[:, 2, 0:n2], zt[:, 2, 0:n2], 1.0, 0.5, ALU.add, ALU.mult).then_inc(sp_step, 1)
        dve.wait_ge(sp_step, 9)
        for j in range(2):
            v.reciprocal(beta_sb[:, j, :, :].rearrange("p h n -> p n h"),
                         zt[:, 2, 0:n2].rearrange("p (n j h) -> p n j h", j=2, h=HEADS)[:, :, j, :]).then_inc(
                sp_step if j == 0 else beta_done, 1)
        dve.wait_ge(sp_step, 10)
        def conv(A, p):
            dve.wait_ge(evac_done, 10 * A.h + p + 1)
            cb = PROJ[p // 2]
            src = bankA[proj_bank(p)][:, :].rearrange("p (b t) -> p b t", b=2)
            for k in range(1, CONV):
                if k > 1:
                    topk(A, 2 * p + k - 2)
                    if some(30 * A.h + 3 * p + k - 1):
                        dve.wait_ge(conv_step, 30 * A.h + 3 * p + k - 1)
                if k < 3:
                    if some(2 * ROUNDS * A.h + 2 * p + k - 1):
                        dve.wait_ge(topk_step, 2 * ROUNDS * A.h + 2 * p + k - 1)
                if k == 1 and p == 0:
                    dve.wait_ge(sim_in[A.par], 16 * (A.use + 1))
                v.scalar_tensor_tensor(out=y[p % 2][:, :, k:], in0=src[:, :, 0:SEQ - k], scalar=cwh[A.par][:, cb, 3 - k:4 - k],
                                       in1=y[p % 2][:, :, k:], op0=ALU.mult, op1=ALU.add).then_inc(conv_step, 1)

        def topk(A, k):
            w = simw[A.par][:, :]
            if k == 2 * ROUNDS - 1:
                at = (TOPK - 1) % 8
                ins = v.tensor_copy(thr[:, A.h:A.h + 1] if isinstance(A.h, int) else thr[:, bass.ds(A.h, 1)], m8[:, at:at + 1])
            elif k % 2 == 0:
                ins = v.max(out=m8[:, :], in_=w)
            else:
                ins = v.match_replace(out=w, in_to_replace=m8[:, :], in_values=w, imm_value=-3.0e38)
            ins.then_inc(topk_step, 1)

        def norm_sum(A, i):
            dve.wait_ge(norm_mm, 6 * A.h + i + 1)
            bank = bankA[norm_bank(i)][:, 0:4]
            if i < 4:
                if i == 0 and some(A.h):
                    dve.wait_ge(kn_done, A.h)
                v.tensor_scalar(ksum[:, 4 * i:4 * i + 4], bank, 1e-24, None, ALU.max).then_inc(sums_done, 1)
            else:
                v.tensor_scalar(qn[:, :, (i - 4) * 4:(i - 3) * 4][:, A.h, :], bank, 1e-24, DH * EPS, ALU.max, ALU.mult).then_inc(sums_done, 1)

        def fold_beta(A):
            if some(A.h):
                dve.wait_ge(dm_done, 2 * A.h)
                dve.wait_ge(sh_done, A.h)
            dve.wait_ge(sums_done, 6 * A.h + 4)
            v.reciprocal(beta_n[:, :], ksum[:, :]).then_inc(beta_step, 1)
            dve.wait_ge(beta_step, 2 * A.h + 1)
            v.tensor_tensor(beta_n[:, :], beta_n[:, :], scal[:, :, 3, :][:, A.h, :], ALU.mult).then_inc(beta_step, 1)

        def evac_b(idx, B):
            kind, n = ITEMS[idx]
            b, lv = n % BATCH, n // BATCH + 1
            if kind not in ("gram", "qk", "kend", "p"):
                return
            dve.wait_ge(b_mm, B_ITEMS * B.h + idx + 1)
            bank = bankB[idx % 4][:, :]
            if kind == "gram":
                if b == 0:
                    dve.wait_ge(dm_done, 2 * B.h + 2)
                v.tensor_tensor(aT[:, b, :, :].rearrange("p c (t j) -> p (c t) j", j=2), bank.rearrange("p (t j) -> p t j", j=2),
                                dx[:, b * CH:(b + 1) * CH, :].rearrange("p c (n a) -> p (c n) a", a=1).to_broadcast([P, CH * STEPS, 2]),
                                ALU.mult).then_inc(at_done, 1)
            elif kind == "qk":
                if b == 0 and (not isinstance(B.h, int) or B.h >= 2):
                    if some(4 * (B.h - 1)):
                        dve.wait_ge(o_mm, 4 * (B.h - 1) + 1)
                v.tensor_tensor(mq[B.par][:, b, :, :].rearrange("p c n -> p (c n)"), bank[:, 0:CH * STEPS],
                                dm[:, b * CH:(b + 1) * CH, :].rearrange("p c n -> p (c n)"), ALU.mult).then_inc(qk_used, 1)
            elif kind == "kend":
                if b == 0:
                    dve.wait_ge(sh_done, B.h + 1)
                v.tensor_tensor(kend[:, b, :, :], bank.rearrange("p (c n) -> p c n", c=CH),
                                sh[B.par][:, 1, b * CH:(b + 1) * CH].rearrange("p (c a) -> p c a", a=1).to_broadcast([P, CH, DH]),
                                ALU.mult).then_inc(kend_done, 1)
            else:
                v.tensor_tensor(Pn[:, b, :, :], bank.rearrange("p (c n) -> p c n", c=CH),
                                mask(f"neg{lv}").rearrange("p (a n) -> p a n", a=1).to_broadcast([P, CH, MU]),
                                ALU.mult).then_inc(p_used, 1)

        def scan(C, slot):
            c, ph = slot // 3, slot % 3
            h, par = C.h, C.par
            if ph == 0 and c > 0:
                if some(3 * h + c):
                    dve.wait_ge(ks_mm, 3 * h + c)
                for b in range(BATCH):
                    v.scalar_tensor_tensor(out=R[:, b, :], in0=bankC[0][:, b * P:(b + 1) * P],
                                           scalar=sh[par][:, 0, b * CH + c:b * CH + c + 1], in1=vtok[par][:, b, c, :],
                                           op0=ALU.mult, op1=ALU.add).then_inc(r_done, 1)
            if ph == 1:
                dve.wait_ge(u_mm, 4 * h + c + 2)
                if c == 0:
                    if some(4 * h):
                        dve.wait_ge(o_mm, 4 * h + 1)
                v.tensor_tensor(U[:, :, :], bankC[1][:, :].rearrange("p (b n) -> p b n", b=BATCH),
                                sh[par][:, 3, :].rearrange("p (b c a) -> p b c a", b=BATCH, a=1)[:, :, c, :].to_broadcast([P, BATCH, DH]),
                                ALU.mult).then_inc(u_done, 1)
            if ph == 2 and c < CH - 1:
                dve.wait_ge(s_mm, 3 * h + c + 1)
                for b in range(BATCH):
                    if c == 0:
                        v.tensor_copy(S[:, b, :], bankC[0][:, b * P:(b + 1) * P]).then_inc(s_done, 1)
                    else:
                        v.scalar_tensor_tensor(out=S[:, b, :], in0=S[:, b, :], scalar=sh[par][:, 2, b * CH + c:b * CH + c + 1],
                                               in1=bankC[0][:, b * P:(b + 1) * P], op0=ALU.mult, op1=ALU.add).then_inc(s_done, 1)

        def out_gate(C):
            dve.wait_ge(osq_done, C.h + 2)
            v.scalar_tensor_tensor(out=og[:, :], in0=oT[:, :, :].rearrange("p b t -> p (b t)"), scalar=normw[:, 0:1],
                                   in1=gate[C.par][:, :], op0=ALU.mult, op1=ALU.mult).then_inc(og_step, 1)

        def out_rms(E):
            dve.wait_ge(oss_mm, E.h + 2)
            v.scalar_tensor_tensor(out=factor[:, :], in0=bankC[0][:, 0:TT_N], scalar=1.0 / DH, in1=qn[:, E.h, :],
                                   op0=ALU.mult, op1=ALU.add).then_inc(osums_done, 1)

        def out_add(E):
            dve.wait_ge(factor_done, E.h + 1)
            for n in range(4):
                dve.wait_ge(wo_mm, 4 * E.h + n + 2)
                for k in range(2):
                    tile = 2 * n + k
                    last = v.scalar_tensor_tensor(out=acc[:, tile, :], in0=bankC[n % 2][:, k * HID:(k + 1) * HID],
                                                  scalar=factor[:, tile:tile + 1], in1=acc[:, tile, :], op0=ALU.mult, op1=ALU.add)
                last.then_inc(acc_done, 1)

        def step(A, B, C, E):
            if B:
                for idx in range(PRE):
                    evac_b(idx, B)
                for b in range(BATCH // 2):
                    diag(nc.vector, dve, B, b)
            if E:
                out_rms(E)
                out_add(E)
            at = PRE
            for slot in range(12):
                if B:
                    for idx in range(at, at + BATCH):
                        evac_b(idx, B)
                    at += BATCH
                if C:
                    scan(C, slot)
                if B and slot % 2 and slot < 11:
                    for idx in range(at, at + BATCH):
                        evac_b(idx, B)
                    at += BATCH
                if A and slot < 10:
                    conv(A, slot)
                if A and slot >= 6:
                    norm_sum(A, slot - 6)
                if A and slot == 9:
                    fold_beta(A)
            if B:
                for idx in range(at, B_ITEMS):
                    evac_b(idx, B)
            if C:
                out_gate(C)

        run_heads(dve, step)

    def gpsimd_program(pool):
        g = nc.gpsimd
        g.memset(zero, 0.0).then_inc(zero_done, 1)
        pool.wait_ge(masks_in, 16)
        pool.wait_ge(small_in, 160)
        pool.wait_ge(scal_done, 4)
        g.tensor_scalar(scal[:, :, 0, :], scal[:, :, 0, :], -1.0, None, ALU.mult).then_inc(scal_done, 1)
        pool.wait_ge(scal_done, 5)

        def start(A):
            h = A.h
            if not isinstance(h, int) or h >= 2:
                if some(30 * (h - 1)):
                    pool.wait_ge(conv_step, 30 * (h - 1))
            g.tensor_copy(cwh[A.par][:, :, :].rearrange("p a k -> p (a k)"),
                          cw[:, :, :, :].rearrange("p h a k -> p h (a k)")[:, h, :]).then_inc(cwh_done, 1)
            if some(4 * h):
                pool.wait_ge(dmat_done, 4 * h)
            g.tensor_tensor(gm[:, :, :], g_sb[:, h, :].rearrange("p (n a) -> p n a", a=1).to_broadcast([STEPS, BC, STEPS]),
                            mask("upto", STEPS).rearrange("p (a n) -> p a n", a=1).to_broadcast([STEPS, BC, STEPS]),
                            ALU.mult).then_inc(gm_done, 1)

        def norm(A):
            pool.wait_ge(sums_done, 6 * A.h + 4)
            if some(4 * A.h):
                pool.wait_ge(vtok_done, 4 * A.h)
            g.tensor_tensor(kn[:, :], ksum[:, :], half.to_broadcast([P, BC]), ALU.pow).then_inc(kn_done, 1)

        def out_rms(E):
            pool.wait_ge(osums_done, E.h + 1)
            g.tensor_tensor(factor[:, :], factor[:, :], minus_half.to_broadcast([P, TT_N]), ALU.pow).then_inc(factor_done, 1)

        def decays(A):
            h = A.h
            pool.wait_ge(dexp_done, 4 * h + 2)
            if some(4 * h):
                pool.wait_ge(qk_used, 4 * h)
            g.tensor_tensor(dm[:, :, :], dx[:, :, :], mask("seen").rearrange("p (a n) -> p a n", a=1).to_broadcast([P, BC, STEPS]),
                            ALU.mult).then_inc(dm_done, 1)

        def fold_beta(A):
            h = A.h
            pool.wait_ge(dm_done, 2 * h + 1)
            pool.wait_ge(beta_step, 2 * h + 2)
            g.tensor_tensor(dx[:, :, :], dx[:, :, :], beta_n[:, :].rearrange("p (n a) -> p n a", a=1).to_broadcast([P, BC, STEPS]),
                            ALU.mult).then_inc(dm_done, 1)

        def scalars(A):
            h = A.h
            if not isinstance(h, int) or h >= 2:
                pool.wait_ge(r_done, 12 * (h - 1))
                pool.wait_ge(u_done, 4 * (h - 1))
                pool.wait_ge(s_done, 12 * (h - 1))
            g.tensor_copy(sh[A.par][:, 0:3, :].rearrange("p a k -> p (a k)"),
                          scal[:, :, 0:3, :].rearrange("p h a k -> p h (a k)")[:, h, :])
            g.tensor_copy(sh[A.par][:, 3, :], beta_n[:, :]).then_inc(sh_done, 1)

        def q_decay(A):
            for i in range(2):
                pool.wait_ge(silu_done, 10 * A.h + 5 + i)
                if i == 0:
                    pool.wait_ge(dexp_done, 4 * A.h + 4)
                    if not isinstance(A.h, int) or A.h >= 2:
                        if some(4 * (A.h - 1)):
                            pool.wait_ge(o_mm, 4 * (A.h - 1) + 1)
                g.tensor_tensor(qE[A.par][:, 2 * i:2 * i + 2, :, :].rearrange("p b c t -> p (b c t)"), qraw[:, i * 512:(i + 1) * 512],
                                ex[:, i * 8:(i + 1) * 8, :].rearrange("p n t -> p (n t)"), ALU.mult).then_inc(qe_done, 1)

        def step(A, B, C, E):
            if A:
                start(A)
            if B:
                for b in range(BATCH // 2, BATCH):
                    diag(nc.gpsimd, pool, B, b)
            if E:
                out_rms(E)
            if A:
                decays(A)
                norm(A)
                fold_beta(A)
                scalars(A)
                q_decay(A)

        run_heads(pool, step)

    return {"sync": sync_program, "pe": tensor_program, "act": scalar_program, "dve": vector_program, "pool": gpsimd_program}


FF = 704
FFH = FF // 2
FT = -(-FF // P)
FT_ROWS = [min(P, FF - k * P) for k in range(FT)]
WAYS = EXPERTS + 1
BACK_EARLY = 8
BASE_FIRST = 6


def feed_forward(nc, t, dram):
    sb, sem, acc, thr = t["sb"], t["sem"], t["acc"], t["thr"]
    gu = t["banks"][0:4]
    tr = t["banks"][4:6]
    dn = t["banks"][6:8]

    masks = sb("f_masks", [P, MASK_W])
    at, _ = MASK_AT["ident"]
    ident = masks[:, at:at + P]
    at, _ = MASK_AT["scal"]
    eps = masks[:, at + 3:at + 4]
    iota = masks[:, at + 8:at + 16]
    ones_m, later = (masks[:, MASK_AT[n][0]:MASK_AT[n][0] + P] for n in ("ones", "strict"))
    tile_no, filled = (masks[:, MASK_AT[n][0]:MASK_AT[n][0] + MASK_AT[n][1]] for n in ("tiles", "filled"))
    stats = sb("f_stats", [P, TT_N, 6])
    mv = sb("f_mv", [P, 2, TT_N, 2])
    lnv = sb("f_lnv", [P, TT_N])
    rstd = sb("f_rstd", [P, 2, TT_N])
    gam = sb("f_gam", [P, 4])
    small = sb("f_small", [P, 4, TT_N])
    gwT = sb("f_gwT", [P, KT_H, EXPERTS])
    gw = sb("f_gw", [EXPERTS, HID])
    lg = sb("f_lg", [P, TT_N, EXPERTS])
    top = sb("f_top", [P, TT_N, 8])
    idx = sb("f_idx", [P, TT_N, 8], mybir.dt.uint32)
    idxf = sb("f_idxf", [P, TT_N, 8])
    hot = sb("f_hot", [P, 2, TT_N, EXPERTS])
    picked = sb("f_picked", [P, 4, TT_N, EXPERTS])
    start = sb("f_start", [P, 4, EXPERTS])
    grid = sb("f_grid", [P, SLOT_TILES, EXPERTS])
    slotf = sb("f_slotf", [P, 2, TT_N])
    slot = sb("f_slot", [P, 2, TT_N], mybir.dt.uint32)
    expf = sb("f_expf", [P, SLOT_TILES])
    expi = sb("f_expi", [P, SLOT_TILES], mybir.dt.int32)
    xg = [sb(f"f_xg{i}", [P, HID]) for i in range(2)]
    xgT = [sb(f"f_xgT{i}", [P, KT_H, P]) for i in range(2)]
    yb = [sb(f"f_yb{i}", [P, HID]) for i in range(2)]
    back = [sb(f"f_back{i}", [P, HID]) for i in range(4)]
    x2T = sb("f_x2T", [P, KT_H, T])
    sg = sb("f_sg", [P, 2, FFH])
    av = sb("f_act", [P, 2, FF])
    aT = sb("f_actT", [P, 2, FT, P])
    wgu = sb("f_wgu", [P, WAYS, KT_H, 2 * FF])
    wdn = sb("f_wdn", [P, WAYS, FT, HID])
    last_w = wgu[:, WAYS - 1, :, :].rearrange("p k n -> p (k n)")
    prev_w = wgu[:, WAYS - 2, :, :].rearrange("p k n -> p (k n)")
    third_w = wgu[:, WAYS - 3, :, :].rearrange("p k n -> p (k n)")
    simb = last_w[:, 0:2048].rearrange("p (n m) -> p n m", n=TT_N)
    am = prev_w[:, 0:2048].rearrange("p (n m) -> p n m", n=TT_N)
    xn2 = third_w[:, 0:2048].rearrange("p (n m) -> p n m", n=TT_N)

    f_in = sem("f_in")
    f_sim_in = sem("f_sim_in")
    f_gw_in = sem("f_gw_in")
    f_sig = sem("f_sig")
    f_gam = sem("f_gam")
    f_am = sem("f_am")
    f_tr_mm = sem("f_tr_mm")
    f_ls = sem("f_ls")
    f_mv = sem("f_mv")
    f_rstd = sem("f_rstd")
    f_x2 = sem("f_x2")
    f_ln2 = sem("f_ln2")
    f_xn2 = sem("f_xn2")
    f_x2t_mm = sem("f_x2t_mm")
    f_x2t = sem("f_x2t")
    f_gwt_mm = sem("f_gwt_mm")
    f_gwt = sem("f_gwt")
    f_lg_mm = sem("f_lg_mm")
    f_route = sem("f_route")
    f_picked = sem("f_picked")
    f_stats = sem("f_stats")
    f_term = sem("f_term")
    f_rank_mm = sem("f_rank_mm")
    f_slots = sem("f_slots")
    f_zero = sem("f_zero")
    f_scattered = sem("f_scattered")
    xg_in = [sem(f"f_xg_in{i}") for i in range(2)]
    y_out = [sem(f"f_y_out{i}") for i in range(2)]
    f_xgt = sem("f_xgt")
    f_y = sem("f_y")
    back_in = [sem(f"f_back_in{i}") for i in range(4)]
    f_back = sem("f_back")
    f_exp = sem("f_exp")
    f_comb = sem("f_comb")
    f_w_landed = sem("f_w_landed")
    f_gu_mm = sem("f_gu_mm")
    f_silu = sem("f_silu")
    f_act = sem("f_act")
    f_at_mm = sem("f_at_mm")
    f_at = sem("f_at")
    f_dn_mm = sem("f_dn_mm")
    f_add = sem("f_add")
    f_out = sem("f_out")
    w_dma = [sem(f"f_w{i}") for i in range(WAYS)]

    def free(eng):
        eng.wait_ge(t["acc_done"], 4 * HEADS + 1)

    def sync_program(sp):
        free(sp)
        sp.dma_start(masks[:, :], dram["masks"]).then_inc(f_in, 16)
        sp.dma_start(gam[:, 0:1], dram["gamma"].rearrange("(a n) -> a n", a=1).to_broadcast([P, 1])).then_inc(f_in, 16)
        sp.dma_start(simb, dram["sim"].rearrange("n p m -> p n m")).then_inc(f_sim_in, 16)
        sp.dma_start(gw[:, :], dram["gate_w"]).then_inc(f_gw_in, 16)
        def fetch(m, par, use):
            if not isinstance(m, int) or m >= 2:
                sp.wait_ge(f_at_mm, 2 * (m + BASE_FIRST) - 6)
            sp.dma_start(xg[par][:, :], dram["slots_x"][m]).then_inc(xg_in[par], 16)

        for e in range(WAYS):
            if e == WAYS - 3:
                sp.wait_ge(f_x2t, 8)
                sp.wait_ge(f_scattered, 32 * TT_N)
                fetch(0, 0, 0)
                fetch(1, 1, 0)
            if e == WAYS - 1:
                fetch(2, 0, 1)
            if e == WAYS - 2:
                sp.wait_ge(f_x2, 2 * TT_N)
            g = dram["base_gu"] if e == 0 else dram["exp_gu"][e - 1]
            d = dram["base_dn"] if e == 0 else dram["exp_dn"][e - 1]
            sp.dma_start(wgu[:, e, :, :], g.rearrange("(k p) n -> p k n", p=P)).then_inc(w_dma[e], 16)
            full = FT - 1
            sp.dma_start(wdn[:, e, 0:full, :], d[0:full * P].rearrange("(k p) n -> p k n", p=P)).then_inc(w_dma[e], 16)
            sp.dma_start(wdn[0:FT_ROWS[-1], e, full, :], d[full * P:FF]).then_inc(w_dma[e], 16)
            if e >= 1:
                sp.wait_ge(w_dma[e - 1], 48)
                sp.sem_inc(f_w_landed, 1)
        sp.wait_ge(w_dma[WAYS - 1], 48)
        sp.sem_inc(f_w_landed, 1)

        def store(m, par):
            sp.wait_ge(f_y, m + 1)
            sp.dma_start(dram["slots_y"][m], yb[par][:, :]).then_inc(y_out[par], 16)

        for par in range(2):
            sp.sem_inc(y_out[par], 1)
        fetch(3, 1, 1)
        with sp.Fori(0, JOBS // 2 - 1) as i:
            store(2 * i, 0)
            fetch(2 * i + 4, 0, i + 2)
            store(2 * i + 1, 1)
            fetch(2 * i + 5, 1, i + 2)
        for m in range(JOBS // 2 * 2 - 2, JOBS):
            store(m, m % 2)
        for n in range(TT_N):
            sp.wait_ge(f_back, 2 * n + 2)
            if n >= BASE_FIRST:
                sp.wait_ge(f_add, n + 1)
            sp.dma_start(dram["out"].rearrange("b s d -> (b s) d")[n * P:(n + 1) * P], acc[:, n, :]).then_inc(f_out, 16)
        sp.wait_ge(f_out, 16 * TT_N)

    def tensor_program(pe):
        mm = nc.tensor.matmul
        free(pe)
        pe.wait_ge(f_in, 32)
        for n in range(TT_N):
            pe.wait_ge(f_am, 2 * (n // 2) + 2)
            if n >= 2:
                if some(n - 1):
                    pe.wait_ge(f_ls, n - 1)
            for k in range(2):
                src = am[:, n // 2 * 2 + k, (n % 2) * P:(n % 2 + 1) * P]
                last = nc.tensor.transpose(tr[n % 2][:, k * P:(k + 1) * P], src, ident)
            last.then_inc(f_tr_mm, 1)
        pe.wait_ge(f_gw_in, 16)
        for k in range(KT_H):
            last = nc.tensor.transpose(dn[0][:, k * EXPERTS:(k + 1) * EXPERTS], gw[:, k * P:(k + 1) * P], ident[0:EXPERTS, 0:EXPERTS])
        last.then_inc(f_gwt_mm, 1)
        for n in range(TT_N):
            pe.wait_ge(f_xn2, n + 1)
            if n < 2:
                if some(TT_N - 1 + n):
                    pe.wait_ge(f_ls, TT_N - 1 + n)
            else:
                if some(n - 1):
                    pe.wait_ge(f_x2t, n - 1)
            for k in range(KT_H):
                last = nc.tensor.transpose(tr[n % 2][:, k * P:(k + 1) * P], xn2[:, n, k * P:(k + 1) * P], ident)
            last.then_inc(f_x2t_mm, 1)
        pe.wait_ge(f_gwt, 1)
        pe.wait_ge(f_x2t, TT_N)
        for n in range(TT_N):
            for k in range(KT_H):
                last = mm(dn[1][:, n * EXPERTS:(n + 1) * EXPERTS], x2T[:, k, n * P:(n + 1) * P], gwT[:, k, :], start=k == 0, stop=k == 1)
        last.then_inc(f_lg_mm, 1)

        def ranks():
            pe.wait_ge(f_picked, 1)
            m = picked[:, 0, :, :].rearrange("p n e -> p (n e)")
            mm(dn[1][:, 64:128], later, m, start=True, stop=True)
            mm(dn[1][:, 128:192], ones_m, m, start=True, stop=True).then_inc(f_rank_mm, 1)

        def gate_up(job, xt, e, part):
            for c in (2 * part, 2 * part + 1):
                at = (c % 2) * FF + (c // 2) * FFH
                if some(job):
                    pe.wait_ge(f_act, 2 * job - 1 + c // 2)
                for k in range(KT_H):
                    last = mm(gu[c][:, 0:FFH], xt[:, k, :], wgu[:, e, k, at:at + FFH], start=k == 0, stop=k == 1)
                last.then_inc(f_gu_mm, 1)

        def base(job, n):
            pe.wait_ge(f_w_landed, 1)
            return lambda part: gate_up(job, x2T[:, :, n * P:(n + 1) * P], 0, part)

        def routed(m, par):
            e = pe.value_load(expi[0:1, m:m + 1] if isinstance(m, int) else expi[0:1, bass.ds(m, 1)], min_val=0, max_val=EXPERTS - 1)
            pe.wait_ge(f_w_landed, e + 2)
            pe.wait_ge(f_xgt, 2 * m + 2)
            return (lambda part: gate_up(m + BASE_FIRST, xgT[par], e + 1, part)), e + 1

        def turn_job(job, par, e, products, turn=None):
            if products:
                products(0)
            pe.wait_ge(f_act, 2 * job + 2)
            for half in range(2):
                if some(job):
                    pe.wait_ge(f_at, 2 * job - 1 + half)
                if turn:
                    if half == 0:
                        pe.wait_ge(xg_in[turn[0]], 16 * (turn[1] + 1))
                    if not turn[2]:
                        pe.wait_ge(f_xgt, 2 * (job + 2 - BASE_FIRST) - 1 + half)
                for k in range(3 * half, 3 * half + 3):
                    rows = FT_ROWS[k]
                    last = nc.tensor.transpose(tr[half][0:rows, (k % 3) * P:(k % 3 + 1) * P], av[:, par, k * P:k * P + rows], ident)
                if turn:
                    last = nc.tensor.transpose(tr[half][:, 3 * P:4 * P], xg[turn[0]][:, half * P:(half + 1) * P], ident)
                last.then_inc(f_at_mm, 1)
            if products:
                products(1)
            if isinstance(job, int) and job == 0:
                pe.wait_ge(f_gwt, 1)
            elif isinstance(job, int) and job == 1:
                pe.wait_ge(f_slots, 1)
            else:
                pe.wait_ge(f_add, job - 1)
            pe.wait_ge(f_at, 2 * job + 2)
            for k in range(FT):
                rows = FT_ROWS[k]
                last = mm(dn[par][:, 0:HID], aT[0:rows, par, k, :], wdn[0:rows, e, k, :], start=k == 0, stop=k == FT - 1)
            last.then_inc(f_dn_mm, 1)

        first = base(0, 0)
        first(0)
        first(1)
        for n in range(BASE_FIRST):
            if n < BASE_FIRST - 1:
                products = base(n + 1, n + 1)
            else:
                products, _ = routed(0, 0)
            if n == 0:
                ranks()
            m = n + 2 - BASE_FIRST
            turn_job(n, n % 2, 0, products, (m % 2, m // 2, m == 0) if m >= 0 else None)
        with pe.Fori(0, JOBS // 2) as i:
            e0 = pe.value_load(expi[0:1, bass.ds(2 * i, 1)], min_val=0, max_val=EXPERTS - 1) + 1
            products, e1 = routed(2 * i + 1, 1)
            turn_job(2 * i + BASE_FIRST, 0, e0, products, (0, i + 1, False))
            products, _ = routed(2 * i + 2, 0)
            turn_job(2 * i + 1 + BASE_FIRST, 1, e1, products, (1, i + 1, False))
        e_last = pe.value_load(expi[0:1, JOBS - 1:JOBS], min_val=0, max_val=EXPERTS - 1) + 1
        turn_job(BASE_FIRST + JOBS - 1, (JOBS - 1) % 2, e_last, base(BASE_FIRST + JOBS, BASE_FIRST))
        for n in range(BASE_FIRST, TT_N):
            turn_job(JOBS + n, (JOBS + n) % 2, 0, base(JOBS + n + 1, n + 1) if n < TT_N - 1 else None)

    def scalar_program(act):
        a = nc.scalar.activation
        free(act)
        act.wait_ge(f_in, 32)
        act.wait_ge(f_sim_in, 16)
        a(am, simb, ACT.Sigmoid, scale=1.0 / 16).then_inc(f_sig, 1)
        a(gam[:, 1:2], gam[:, 0:1], ACT.Sigmoid).then_inc(f_gam, 1)
        nc.scalar.preload_act_table_set(LN_EXP)

        def inv_std(i):
            if some(TT_N * (i + 1)):
                act.wait_ge(f_mv, TT_N * (i + 1))
            a(lnv[:, :], mv[:, i, :, 1], ACT.Ln, bias=eps).then_inc(f_rstd, 1)
            act.wait_ge(f_rstd, 2 * i + 1)
            a(rstd[:, i, :], lnv[:, :], ACT.Exp, scale=-0.5).then_inc(f_rstd, 1)

        inv_std(0)
        act.wait_ge(f_gwt_mm, 1)
        a(gwT[:, :, :].rearrange("p k n -> p (k n)"), dn[0][:, 0:KT_H * EXPERTS], ACT.Copy).then_inc(f_gwt, 1)
        inv_std(1)
        for n in range(TT_N):
            act.wait_ge(f_x2t_mm, n + 1)
            a(x2T[:, :, n * P:(n + 1) * P], tr[n % 2][:, 0:HID].rearrange("p (k c) -> p k c", k=KT_H), ACT.Copy).then_inc(f_x2t, 1)
        act.wait_ge(f_route, 1)
        a(small[:, 1, :], small[:, 0, :], ACT.Exp).then_inc(f_exp, 1)

        def silu(job, half):
            act.wait_ge(f_gu_mm, 4 * job + 2 * half + 1)
            if some(job):
                act.wait_ge(f_act, 2 * job - 1 + half)
            a(sg[:, half, :], gu[2 * half][:, 0:FFH], ACT.Silu).then_inc(f_silu, 1)

        def copy_t(job, par, turn=None):
            if not isinstance(job, int) or job >= 2:
                act.wait_ge(f_dn_mm, job - 1)
            for half in range(2):
                act.wait_ge(f_at_mm, 2 * job + half + 1)
                if turn is not None:
                    a(xgT[turn][:, half, :], tr[half][:, 3 * P:4 * P], ACT.Copy).then_inc(f_xgt, 1)
                if half == 0:
                    a(aT[:, par, 0:3, :].rearrange("p k c -> p (k c)"), tr[0][:, 0:3 * P], ACT.Copy).then_inc(f_at, 1)
                else:
                    a(aT[:, par, 3:5, :].rearrange("p k c -> p (k c)"), tr[1][:, 0:2 * P], ACT.Copy)
                    a(aT[0:FT_ROWS[-1], par, 5, :], tr[1][0:FT_ROWS[-1], 2 * P:3 * P], ACT.Copy).then_inc(f_at, 1)

        def turn_job(job, par, turn=None):
            silu(job + 1, 0)
            copy_t(job, par, turn)
            silu(job + 1, 1)

        silu(0, 0)
        silu(0, 1)
        for n in range(BASE_FIRST):
            turn_job(n, n % 2, n % 2 if n >= BASE_FIRST - 2 else None)
        with act.Fori(0, JOBS // 2) as i:
            turn_job(2 * i + BASE_FIRST, 0, 0)
            turn_job(2 * i + 1 + BASE_FIRST, 1, 1)
        for job in range(BASE_FIRST + JOBS - 1, TT_N + JOBS - 1):
            turn_job(job, job % 2)
        copy_t(TT_N + JOBS - 1, (TT_N + JOBS - 1) % 2)

    def vector_program(dve):
        v = nc.vector
        free(dve)
        chain = sem("f_chain")
        count = [0]

        def link(ins):
            count[0] += 1
            ins.then_inc(chain, 1)
            dve.wait_ge(chain, count[0])

        def moments(i):
            for n in range(TT_N):
                if i:
                    dve.wait_ge(f_x2, 2 * n + 2)
                v.bn_stats(stats[:, n, :], acc[:, n, :]).then_inc(f_stats, 1)
            for n in range(TT_N):
                dve.wait_ge(f_stats, TT_N * i + n + 1)
                v.bn_aggr(mv[:, i, n, :], stats[:, n, :]).then_inc(f_mv, 1)

        moments(0)
        dve.wait_ge(f_gam, 1)
        link(v.tensor_scalar(gam[:, 2:3], gam[:, 1:2], 0.5, None, ALU.mult))
        link(v.tensor_scalar(gam[:, 3:4], gam[:, 1:2], -1.0, 1.0, ALU.mult, ALU.add))
        dve.wait_ge(f_sig, 1)
        for n in range(TT_N):
            v.scalar_tensor_tensor(out=am[:, n, :], in0=simb[:, n, :], scalar=thr[:, n:n + 1], in1=am[:, n, :], op0=ALU.is_ge,
                                   op1=ALU.mult).then_inc(f_am, 1)
        dve.wait_ge(f_am, TT_N)
        for n in range(TT_N):
            dve.wait_ge(f_tr_mm, n + 1)
            v.tensor_tensor(simb[:, n, :], am[:, n, :], tr[n % 2][:, 0:SEQ], ALU.add).then_inc(f_ls, 1)
        dve.wait_ge(f_ls, TT_N)
        dve.wait_ge(f_rstd, 2)
        link(v.tensor_scalar(small[:, 0, :], rstd[:, 0, :], gam[:, 3:4], None, ALU.mult))
        link(v.tensor_tensor(small[:, 2, :], small[:, 0, :], mv[:, 0, :, 0], ALU.mult))
        for n in range(TT_N):
            v.tensor_scalar(xn2[:, n, :], acc[:, n, :], mv[:, 0, n, 0:1], small[:, 0, n:n + 1], ALU.subtract, ALU.mult).then_inc(f_term, 1)
        for n in range(TT_N):
            dve.wait_ge(f_term, n + 1)
            v.scalar_tensor_tensor(out=xn2[:, n, :], in0=simb[:, n, :], scalar=gam[:, 2:3], in1=xn2[:, n, :], op0=ALU.mult,
                                   op1=ALU.add).then_inc(f_term, 1)
        for n in range(TT_N):
            dve.wait_ge(f_term, TT_N + n + 1)
            v.tensor_tensor(acc[:, n, :], acc[:, n, :], xn2[:, n, :], ALU.add).then_inc(f_x2, 2)
        moments(1)
        dve.wait_ge(f_mv, 2 * TT_N)
        dve.wait_ge(f_rstd, 4)
        for n in range(TT_N):
            v.tensor_scalar(xn2[:, n, :], acc[:, n, :], mv[:, 1, n, 0:1], rstd[:, 1, n:n + 1], ALU.subtract, ALU.mult).then_inc(f_xn2, 1)
        def choose():
            dve.wait_ge(f_lg_mm, 1)
            link(v.tensor_copy(lg[:, :, :].rearrange("p n e -> p (n e)"), dn[1][:, 0:TT_N * EXPERTS]))
            for n in range(TT_N):
                last = v.max(out=top[:, n, :], in_=lg[:, n, :])
            link(last)
            v.tensor_tensor(small[:, 0, :], top[:, :, 1], top[:, :, 0], ALU.subtract).then_inc(f_route, 1)
            for n in range(TT_N):
                last = v.max_index(out=idx[:, n, :], in_max=top[:, n, :], in_values=lg[:, n, :])
            link(last)
            link(v.tensor_copy(idxf[:, :, :].rearrange("p n e -> p (n e)"), idx[:, :, :].rearrange("p n e -> p (n e)")))
            io = iota.rearrange("p (a e) -> p a e", a=1).to_broadcast([P, TT_N, EXPERTS])
            for j in range(2):
                last = v.tensor_tensor(hot[:, j, :, :], io, idxf[:, :, j:j + 1].to_broadcast([P, TT_N, EXPERTS]), ALU.is_equal)
            link(last)
            v.tensor_tensor(picked[:, 0, :, :], hot[:, 0, :, :], hot[:, 1, :, :], ALU.add).then_inc(f_picked, 1)

        def weigh():
            dve.wait_ge(f_exp, 1)
            link(v.tensor_scalar(small[:, 2, :], small[:, 1, :], 1.0, None, ALU.add))
            link(v.reciprocal(small[:, 2, :], small[:, 2, :]))
            link(v.tensor_tensor(small[:, 3, :], small[:, 1, :], small[:, 2, :], ALU.mult))

        def place():
            dve.wait_ge(f_rank_mm, 1)
            whole = picked[:, 2, :, :]
            link(v.tensor_copy(picked[:, 1:3, :, :].rearrange("p i n e -> p (i n e)"), dn[1][:, 64:192]))
            before = picked[:, 3, :, :]
            link(v.memset(before[:, 0, :], 0.0))
            for n in range(1, TT_N):
                link(v.tensor_tensor(before[:, n, :], before[:, n - 1, :], whole[:, n - 1, :], ALU.add))
            counts, tiles, ends, begin = (start[:, i, :] for i in range(4))
            link(v.tensor_tensor(counts, before[:, TT_N - 1, :], whole[:, TT_N - 1, :], ALU.add))
            link(v.tensor_tensor(grid[:, 0:EXPERTS, :], counts.rearrange("p (e a) -> p e a", a=1).to_broadcast([P, EXPERTS, TT_N]),
                                 filled.rearrange("p (a k) -> p a k", a=1).to_broadcast([P, EXPERTS, TT_N]), ALU.is_gt))
            link(v.tensor_reduce(out=tiles, in_=grid[:, 0:EXPERTS, :], axis=mybir.AxisListType.X, op=ALU.add))
            link(v.tensor_copy(ends[:, 0:1], tiles[:, 0:1]))
            for e in range(1, EXPERTS):
                link(v.tensor_tensor(ends[:, e:e + 1], ends[:, e - 1:e], tiles[:, e:e + 1], ALU.add))
            link(v.tensor_tensor(begin, ends, tiles, ALU.subtract))
            link(v.tensor_tensor(grid[:, :, :], ends.rearrange("p (a e) -> p a e", a=1).to_broadcast([P, SLOT_TILES, EXPERTS]),
                                 tile_no.rearrange("p (m a) -> p m a", a=1).to_broadcast([P, SLOT_TILES, EXPERTS]), ALU.is_le))
            link(v.tensor_reduce(out=expf[:, :], in_=grid[:, :, :], axis=mybir.AxisListType.X, op=ALU.add))
            link(v.tensor_scalar(expi[:, :], expf[:, :], float(EXPERTS - 1), None, ALU.min))
            link(v.tensor_tensor(before, before, picked[:, 1, :, :], ALU.add))
            link(v.tensor_scalar(begin, begin, float(P), None, ALU.mult))
            link(v.tensor_tensor(before, before, begin.rearrange("p (a e) -> p a e", a=1).to_broadcast([P, TT_N, EXPERTS]), ALU.add))
            for j in range(2):
                link(v.tensor_tensor(hot[:, j, :, :], hot[:, j, :, :], before, ALU.mult))
                link(v.tensor_reduce(out=slotf[:, j, :], in_=hot[:, j, :, :], axis=mybir.AxisListType.X, op=ALU.add))
            v.tensor_copy(slot[:, :, :].rearrange("p j n -> p (j n)"), slotf[:, :, :].rearrange("p j n -> p (j n)")).then_inc(f_slots, 1)

        def gated(job, par):
            for half in range(2):
                dve.wait_ge(f_silu, 2 * job + half + 1)
                dve.wait_ge(f_gu_mm, 4 * job + 2 * half + 2)
                if half == 0 and not (isinstance(job, int) and job < 2):
                    dve.wait_ge(f_at_mm, 2 * job - 2)
                v.tensor_tensor(av[:, par, half * FFH:(half + 1) * FFH], sg[:, half, :], gu[2 * half + 1][:, 0:FFH],
                                ALU.mult).then_inc(f_act, 1)

        def add_base(job, n):
            dve.wait_ge(f_dn_mm, job + 1)
            v.tensor_tensor(acc[:, n, :], dn[job % 2][:, 0:HID], acc[:, n, :], ALU.add).then_inc(f_add, 1)

        def keep_routed(m, par, use):
            dve.wait_ge(f_dn_mm, m + BASE_FIRST + 1)
            dve.wait_ge(y_out[par], 16 * use + 1)
            v.tensor_copy(yb[par][:, :], dn[par][:, 0:HID]).then_inc(f_y, 1)
            dve.wait_ge(f_y, m + 1)
            dve.sem_inc(f_add, 1)

        def add_back(k):
            n, j = k // 2, k % 2
            dve.wait_ge(back_in[k % 4], 16 * (k // 4 + 1))
            if some(k):
                dve.wait_ge(f_back, k)
            v.scalar_tensor_tensor(out=acc[:, n, :], in0=back[k % 4][:, :], scalar=small[:, 2 + j, n:n + 1], in1=acc[:, n, :],
                                   op0=ALU.mult, op1=ALU.add).then_inc(f_back, 1)

        choose()
        gated(0, 0)
        weigh()
        place()
        for n in range(BASE_FIRST):
            gated(n + 1, (n + 1) % 2)
            add_base(n, n)
        with dve.Fori(0, JOBS // 2) as i:
            gated(2 * i + 1 + BASE_FIRST, 1)
            keep_routed(2 * i, 0, i)
            gated(2 * i + 2 + BASE_FIRST, 0)
            keep_routed(2 * i + 1, 1, i)
        gated(BASE_FIRST + JOBS, (BASE_FIRST + JOBS) % 2)
        keep_routed(JOBS - 1, (JOBS - 1) % 2, (JOBS - 1) // 2)
        late = TT_N - BASE_FIRST
        for i in range(late):
            job = JOBS + BASE_FIRST + i
            if i < late - 1:
                gated(job + 1, (job + 1) % 2)
            add_base(job, BASE_FIRST + i)
            if i == late - 2:
                dve.wait_ge(f_add, job)
                for k in range(BACK_EARLY):
                    add_back(k)
        dve.wait_ge(f_add, TT_N + JOBS)
        for k in range(BACK_EARLY, 2 * TT_N):
            add_back(k)

    def gpsimd_program(pool):
        g = nc.gpsimd
        rows_x = dram["slots_x"].rearrange("m p d -> (m p) d")
        rows_y = dram["slots_y"].rearrange("m p d -> (m p) d")
        pool.wait_ge(t["slots_zeroed"], 16 * SLOT_TILES)
        pool.wait_ge(f_xn2, TT_N)
        pool.wait_ge(f_slots, 1)
        for n in range(TT_N):
            for j in range(2):
                g.indirect_dma_start(out=rows_x, out_offset=bass.IndirectOffsetOnAxis(ap=slot[:, j, n:n + 1], axis=0),
                                     in_=xn2[:, n, :], in_offset=None).then_inc(f_scattered, 16)
        pool.wait_ge(y_out[0], 16 * ((JOBS + 1) // 2) + 1)
        pool.wait_ge(y_out[1], 16 * (JOBS // 2) + 1)
        for k in range(2 * TT_N):
            if k >= 4:
                pool.wait_ge(f_back, k - 3)
            g.indirect_dma_start(out=back[k % 4][:, :], out_offset=None, in_=rows_y,
                                 in_offset=bass.IndirectOffsetOnAxis(ap=slot[:, k % 2, k // 2:k // 2 + 1], axis=0)).then_inc(back_in[k % 4], 16)

    return {"sync": sync_program, "pe": tensor_program, "act": scalar_program, "dve": vector_program, "pool": gpsimd_program}


def build(nc, dram):
    with ExitStack() as ctx:
        t = {}
        t["sem"] = lambda name: ctx.enter_context(nc.semaphore(name))
        t["banks"] = [ctx.enter_context(nc.psum_tensor(f"bank{i}", [P, 512], F32)) for i in range(8)]
        keep = lambda name, shape, dt=F32: ctx.enter_context(nc.sbuf_tensor(name, shape, dt))
        t["acc"] = keep("acc", [P, TT_N, HID])
        t["thr"] = keep("thr", [P, TT_N])
        with ExitStack() as first:
            t["sb"] = lambda name, shape, dt=F32: first.enter_context(nc.sbuf_tensor(name, shape, dt))
            one = attention(nc, first, t, dram)
        t["sb"] = keep
        two = feed_forward(nc, t, dram)
        block = ctx.enter_context(nc.Block())

        @block.sync
        def _(sp):
            one["sync"](sp)
            two["sync"](sp)

        @block.tensor
        def _(pe):
            one["pe"](pe)
            two["pe"](pe)

        @block.scalar
        def _(act):
            one["act"](act)
            two["act"](act)

        @block.vector
        def _(dve):
            one["dve"](dve)
            two["dve"](dve)

        @block.gpsimd
        def _(pool):
            one["pool"](pool)
            two["pool"](pool)


NAMES = {"x": "x", "ctx": "ctx_512", "Wcq": "L0_xattn_Wq", "Wck": "L0_xattn_Wk", "gamma": "L0_xattn_gamma_raw",
         "Wq": "L0_attn_Wq", "Wk": "L0_attn_Wk", "Wv": "L0_attn_Wv", "Wb": "L0_attn_Wb", "Wa": "L0_attn_Wa",
         "A_log": "L0_attn_A_log", "dt_bias": "L0_attn_dt_bias", "cq": "L0_attn_conv_q_w", "ck": "L0_attn_conv_k_w",
         "cv": "L0_attn_conv_v_w", "Wg": "L0_attn_Wg", "norm_w": "L0_attn_norm_w", "Wo": "L0_attn_Wo",
         "gate_w": "L0_ffn_gate_w", "base_gu": "L0_ffn_base_gate_up", "base_dn": "L0_ffn_base_down",
         "exp_gu": "L0_ffn_expert_gate_up", "exp_dn": "L0_ffn_expert_down"}


def kernel(**inputs):
    import numpy as _np
    import concourse.bacc as _bacc
    from concourse import mybir as _mybir
    from concourse.bass_utils import run_bass_kernel_spmd as _run

    nc = _bacc.Bacc("TRN2", target_bir_lowering=False, num_devices=1)
    arrays, dram = {}, {}
    for short, name in NAMES.items():
        a = _np.ascontiguousarray(inputs[name])
        if a.ndim == 0:
            a = a.reshape(1)
        arrays[f"in_{short}"] = a
        dram[short] = nc.dram_tensor(f"in_{short}", a.shape, _mybir.dt.from_np(a.dtype), kind="ExternalInput").ap()
    table = _np.concatenate([MASKS[k] for k in MASKS], axis=1)
    arrays["in_masks"] = table
    dram["masks"] = nc.dram_tensor("in_masks", table.shape, F32, kind="ExternalInput").ap()
    dram["sim"] = nc.dram_tensor("similarities", (TT_N, P, SEQ), F32, kind="Internal").ap()
    dram["slots_x"] = nc.dram_tensor("slots_x", (SLOT_TILES, P, HID), F32, kind="Internal").ap()
    dram["slots_y"] = nc.dram_tensor("slots_y", (JOBS, P, HID), F32, kind="Internal").ap()
    dram["out"] = nc.dram_tensor("out_0", (BATCH, SEQ, HID), F32, kind="ExternalOutput").ap()
    build(nc, dram)
    r = _run(nc, [arrays], core_ids=[0])
    return r.results[0]["out_0"]
```
